# Optimizing a Trainium2 kernel written in Bass

```python
import numpy as np
import jax
import jax.numpy as jnp

def _softmax(x, axis=-1):
    return jax.nn.softmax(x, axis=axis)

def _gelu(x):
    return jax.nn.gelu(x, approximate=True)

def _silu(x):
    return jax.nn.silu(x)

def _sigmoid(x):
    return jax.nn.sigmoid(x)

def _layernorm(x, axis=-1, eps=1e-05):
    m = jnp.mean(x, axis=axis, keepdims=True)
    v = jnp.var(x, axis=axis, keepdims=True)
    return (x - m) / jnp.sqrt(v + eps)

def _scatter_add(tgt, idx, src, axis=0):
    return tgt.at[idx].add(src)

def _segment_sum(src, seg, n):
    return jax.ops.segment_sum(src, seg, n)
kernel_name = 'mk_seq_preln_d1_jaxref_r8_f9bb3d'

def setup_inputs(seed: int=0):
    np.random.seed(seed)
    _w = jnp.asarray

    def _L0_attn_setup():
        import jax, jax.numpy as jnp
        import numpy as np
        B, T, D, W = (2, 1024, 256, 128)
        PAD = -1.0
        key = jax.random.key(seed)
        k1, k2, k3 = jax.random.split(key, 3)
        x = jax.random.normal(k1, (B, T, D), jnp.float32)
        w_attn = jax.random.normal(k2, (3 * D, D), jnp.float32) * 0.02
        w_o = jax.random.normal(k3, (D, D), jnp.float32) * 0.02
        return {'x': x, 'w_attn': w_attn, 'w_o': w_o}
    _L0_attn_in = _L0_attn_setup()

    def _L0_ffn_setup():
        import jax, jax.numpy as jnp
        import numpy as np
        EPS = 1e-08

        def _quantize(w):
            gamma = jnp.mean(jnp.abs(w))
            return jnp.clip(jnp.round(w / (gamma + EPS)), -1.0, 1.0)

        def _bitlinear(x, w):
            return jnp.matmul(x, _quantize(w).T)
        key = jax.random.key(seed)
        k1, k2, k3, k4 = jax.random.split(key, 4)
        d, h = (256, 704)
        x = jax.random.normal(k1, (4, 256, d), dtype=jnp.float32)
        w1 = jax.random.normal(k2, (h, d), dtype=jnp.float32)
        w2 = jax.random.normal(k3, (h, d), dtype=jnp.float32)
        w3 = jax.random.normal(k4, (d, h), dtype=jnp.float32)
        return {'x': x, 'w1': w1, 'w2': w2, 'w3': w3}
    _L0_ffn_in = _L0_ffn_setup()
    _d = {'L0_attn_x': _L0_attn_in['x'], 'L0_attn_w_attn': _L0_attn_in['w_attn'], 'L0_attn_w_o': _L0_attn_in['w_o'], 'L0_ffn_w1': _L0_ffn_in['w1'], 'L0_ffn_w2': _L0_ffn_in['w2'], 'L0_ffn_w3': _L0_ffn_in['w3']}
    _x0 = _d['L0_attn_x']
    _d['L0_attn_x'] = jax.random.normal(jax.random.fold_in(jax.random.key(seed), 1), (8, 512, 256), dtype=_x0.dtype)
    del _x0
    return _d

def reference(L0_attn_x, L0_attn_w_attn, L0_attn_w_o, L0_ffn_w1, L0_ffn_w2, L0_ffn_w3):

    def _L0_attn_ref(x, w_attn, w_o):
        import jax, jax.numpy as jnp
        import numpy as np
        B, T, D, W = (2, 1024, 256, 128)
        PAD = -1.0
        Bn, Tn, Dn = x.shape
        w = Tn // W
        qkv = x @ w_attn.T
        q, k, v = jnp.split(qkv, 3, axis=-1)
        q = q / W
        bq = q.reshape(Bn, w, W, Dn)
        bk = k.reshape(Bn, w, W, Dn)
        bv = v.reshape(Bn, w, W, Dn)
        pad_blk = jnp.full((Bn, 1, W, Dn), PAD, dtype=x.dtype)
        bk_prev = jnp.concatenate([pad_blk, bk[:, :-1]], axis=1)
        bv_prev = jnp.concatenate([pad_blk, bv[:, :-1]], axis=1)
        bk2 = jnp.concatenate([bk_prev, bk], axis=2)
        bv2 = jnp.concatenate([bv_prev, bv], axis=2)
        t = jnp.arange(Tn, dtype=jnp.int32).reshape(w, W)
        t_prev = jnp.concatenate([jnp.full((1, W), -1, jnp.int32), t[:-1]], axis=0)
        tj = jnp.concatenate([t_prev, t], axis=1)
        ti = t[:, :, None]
        tjb = tj[:, None, :]
        keep = (ti >= tjb) & (ti <= tjb + W) & (tjb != -1)
        sim = jnp.einsum('bwie,bwje->bwij', bq, bk2)
        sim = jnp.where(keep[None], sim, 0.0)
        attn = jnp.square(jax.nn.relu(sim))
        out = jnp.einsum('bwij,bwje->bwie', attn, bv2)
        out = out.reshape(Bn, Tn, Dn)
        return out @ w_o.T

    def _L0_ffn_ref(x, w1, w2, w3):
        import jax, jax.numpy as jnp
        import numpy as np
        EPS = 1e-08

        def _quantize(w):
            gamma = jnp.mean(jnp.abs(w))
            return jnp.clip(jnp.round(w / (gamma + EPS)), -1.0, 1.0)

        def _bitlinear(x, w):
            return jnp.matmul(x, _quantize(w).T)
        x1 = _bitlinear(x, w1)
        x2 = _bitlinear(x, w2)
        hidden = jax.nn.sigmoid(x1) * x2
        return _bitlinear(hidden, w3)
    x = L0_attn_x
    x = x + _L0_attn_ref(_layernorm(x, axis=-1), L0_attn_w_attn, L0_attn_w_o)
    x = x + _L0_ffn_ref(_layernorm(x, axis=-1), L0_ffn_w1, L0_ffn_w2, L0_ffn_w3)
    return x

_drawn_inputs = setup_inputs


def setup_inputs(seed=0):
    import zlib

    import numpy as np

    out = dict(_drawn_inputs(seed))
    spreads = {}
    factors = {'L0_attn_w_attn': 8.0, 'L0_attn_w_o': 8.0}
    for name, (base, spread) in spreads.items():
        noise = np.random.default_rng([zlib.crc32(name.encode()), seed]).standard_normal(out[name].shape)
        drawn = base * np.exp(spread * noise) if base else spread * noise
        out[name] = jnp.asarray(drawn.astype(out[name].dtype))
    for name, factor in factors.items():
        out[name] = (out[name] * factor).astype(out[name].dtype)
    return out
```

```python
from contextlib import ExitStack

import concourse.bass as bass
from concourse import mybir

P = 128
F32 = mybir.dt.float32
F32R = mybir.dt.float32r
BF16 = mybir.dt.bfloat16
ALU = mybir.AluOpType
ACT = mybir.ActivationFunctionType
AX_X = mybir.AxisListType.X

LN_EPS = 1e-5
QUANT_EPS = 1e-8
BIG = 3.4028234663852886e38

XT, ZT, UV, SC, YA, X2T = 0, 2, 4, 6, 8, 10
A_USES = 12


def build(nc, x, w_attn, w_o, w1, w2, w3, out):
    B, T, D = x.shape
    H = w1.shape[0]
    NB = T // P
    KD = D // P
    HC = H // P
    TAIL = H - HC * P
    assert NB == 4 and KD == 2 and TAIL == 64 and T == 512
    XB = NB * D
    NCH = 2 * HC + 1
    UP_ORDER = [0, 1, 2, HC, 3, 4]
    NU = len(UP_ORDER)
    RED = 64
    PS = 24
    WINDOW = float(P)

    x_dram = x.rearrange("b (j p) d -> p b j d", p=P)
    out_dram = out.rearrange("b (j p) d -> p b j d", p=P)

    with ExitStack() as ctx:
        def sb(name, shape, dt=F32):
            return ctx.enter_context(nc.sbuf_tensor(name, shape, dt))

        def bank(name):
            return ctx.enter_context(nc.psum_tensor(name, [P, 512], F32))

        def sem(name):
            return ctx.enter_context(nc.semaphore(name))

        xs = sb("xs", [P, B * XB])
        wat = sb("wat", [P, 3 * KD, D])
        wo_n = sb("wo_n", [P, KD, D])
        woT = sb("woT", [P, KD, D])
        w12_n = sb("w12_n", [P, NCH, D])
        w3_n = sb("w3_n", [P, KD, H])
        m_hi, m_lo = sb("m_hi", [P, KD, D], F32R), sb("m_lo", [P, KD, D], F32R)
        wvo_hi, wvo_lo = sb("wvo_hi", [P, KD, D], F32R), sb("wvo_lo", [P, KD, D], F32R)
        above12, below12 = sb("above12", [P, NCH, D], BF16), sb("below12", [P, NCH, D], BF16)
        H3 = (HC + 1) * P
        above3, below3 = sb("above3", [P, KD, H3], BF16), sb("below3", [P, KD, H3], BF16)
        w12T = sb("w12T", [P, KD, NCH, P], F32R)
        w3T = sb("w3T", [P, HC + 1, D], F32R)
        abs_part = sb("abs_part", [P, 3 * PS])
        abs_total = sb("abs_total", [P, 3])
        thr, nthr = sb("thr", [P, 4]), sb("nthr", [P, 4])
        ident = sb("ident", [P, P])
        ident_bf, nident_bf = sb("ident_bf", [P, P], BF16), sb("nident_bf", [P, P], BF16)
        ones = sb("ones", [P, P])
        neg_half = sb("neg_half", [P, NB])
        cap01 = sb("cap01", [P, 2, 2, P])
        cap23 = sb("cap23", [P, 3, P])

        stats1, stats2 = sb("stats1", [P, NB, 6]), sb("stats2", [P, NB, 6])
        mv1, mv2 = sb("mv1", [P, NB, 2]), sb("mv2", [P, NB, 2])
        veps1, veps2 = sb("veps1", [P, NB]), sb("veps2", [P, NB])
        rstd1, rstd2 = sb("rstd1", [P, NB]), sb("rstd2", [P, NB])
        xn1, xn2 = sb("xn1", [P, NB, D]), sb("xn2", [P, NB, D])
        xT_hi, xT_lo = sb("xT_hi", [P, KD, T], F32R), sb("xT_lo", [P, KD, T], F32R)
        x2T_hi, x2T_lo = sb("x2T_hi", [P, KD, T], F32R), sb("x2T_lo", [P, KD, T], F32R)
        z_hi, z_lo = sb("z_hi", [P, KD, T], F32R), sb("z_lo", [P, KD, T], F32R)
        u_hi, u_lo = sb("u_hi", [P, NB, D], F32R), sb("u_lo", [P, NB, D], F32R)
        sc_pos = sb("sc_pos", [P, 2, 512])
        sc_sq = sb("sc_sq", [P, 2, 512])
        at_hi, at_lo = sb("at_hi", [P, 2, 512], F32R), sb("at_lo", [P, 2, 512], F32R)
        gate = sb("gate", [P, 2, T])
        hid = sb("hid", [P, 2, T])
        hid_hi, hid_lo = sb("hid_hi", [P, HC, T], F32R), sb("hid_lo", [P, HC, T], F32R)
        tail_hi = sb("tail_hi", [TAIL, T], F32R)
        tail_st = sb("tail_st", [P, T], F32R)

        a_bank = [bank("a_bank0"), bank("a_bank1")]
        up_bank = [[bank(f"up{r}_{g}") for g in range(2)] for r in range(2)]
        d_bank = [bank("d_bank0"), bank("d_bank1")]
        prep_bank = [up_bank[0][0], up_bank[0][1], up_bank[1][0], up_bank[1][1]]

        x_loaded = sem("x_loaded")
        wat_loaded, wo_loaded = sem("wat_loaded"), sem("wo_loaded")
        w1_loaded, w2_loaded, w3_loaded = sem("w1_loaded"), sem("w2_loaded"), sem("w3_loaded")
        zeroed, consts_ready, caps_ready = sem("zeroed"), sem("consts_ready"), sem("caps_ready")
        comp_full = sem("comp_full")
        comp_hi, comp_done = sem("comp_hi"), sem("comp_done")
        wo_turned = sem("wo_turned")
        part_zeroed, part_ready = sem("part_zeroed"), sem("part_ready")
        total_ready, thr_ready, ternary_ready = sem("total_ready"), sem("thr_ready"), sem("ternary_ready")
        prep_full, prep_drained = sem("prep_full"), sem("prep_drained")
        stats1_done, mv1_ready, veps1_ready, rstd1_ready, xn1_ready = (
            sem("stats1_done"), sem("mv1_ready"), sem("veps1_ready"), sem("rstd1_ready"), sem("xn1_ready"))
        stats2_done, mv2_ready, veps2_ready, rstd2_ready, xn2_ready = (
            sem("stats2_done"), sem("mv2_ready"), sem("veps2_ready"), sem("rstd2_ready"), sem("xn2_ready"))
        a_full = sem("a_full")
        a_hi = sem("a_hi")
        a_drained = sem("a_drained")
        sq_ready, at_hi_ready, at_lo_ready = sem("sq_ready"), sem("at_hi_ready"), sem("at_lo_ready")
        up_full, gate_ready = sem("up_full"), sem("gate_ready")
        hid_ready = sem("hid_ready")
        hid_hi_ready, hid_lo_ready = sem("hid_hi_ready"), sem("hid_lo_ready")
        d_full, out_ready = sem("d_full"), sem("out_ready")
        stored = sem("stored")
        waits_alone = sem("waits_alone")

        block = ctx.enter_context(nc.Block())

        def wait_alone(eng, what, count):
            eng.wait_ge(what, count)
            eng.sem_inc(waits_alone, 1)

        def xblk(b, j, n=1):
            return xs[:, bass.ds(b * XB + j * D, n * D)]

        @block.sync
        def _(sp):
            sp.dma_start(xblk(0, 0, NB).rearrange("p (j d) -> p j d", j=NB), x_dram[:, 0]).then_inc(x_loaded, 16)
            sp.dma_start(w12_n[:, 0:HC, :], w1[0:HC * P, :].rearrange("(c p) d -> p c d", p=P)).then_inc(w1_loaded, 16)
            sp.dma_start(w12_n[TAIL:P, 2 * HC, :], w1[HC * P:H, :]).then_inc(w1_loaded, 16)
            sp.dma_start(w12_n[:, HC:2 * HC, :], w2[0:HC * P, :].rearrange("(c p) d -> p c d", p=P)).then_inc(w2_loaded, 16)
            sp.dma_start(w12_n[0:TAIL, 2 * HC, :], w2[HC * P:H, :]).then_inc(w2_loaded, 16)
            sp.dma_start(w3_n[:, :, :], w3.rearrange("(c p) h -> p c h", p=P)).then_inc(w3_loaded, 16)
            with sp.Fori(1, B) as i:
                sp.wait_ge(x_loaded, 16 * i)
                dst = xs[:, bass.ds(i * XB, XB)].rearrange("p (j d) -> p j d", j=NB)
                src = x_dram[:, bass.ds(i, 1)].rearrange("p o j d -> p (o j) d")
                sp.dma_start(dst, src).then_inc(x_loaded, 16)
            with sp.Fori(0, B) as i:
                sp.wait_ge(out_ready, 2 * i + 2)
                dst = out_dram[:, bass.ds(i, 1)].rearrange("p o j d -> p (o j) d")
                src = xs[:, bass.ds(i * XB, XB)].rearrange("p (j d) -> p j d", j=NB)
                sp.dma_start(dst, src).then_inc(stored, 16)
            sp.wait_ge(stored, 16 * B)

        @block.tensor
        def _(pe):
            def a_take(b, use, need=0):
                least = max(need, use - 1)
                if not (isinstance(b, int) and b * A_USES + least <= 0):
                    pe.wait_ge(a_drained, b * A_USES + least)
                return a_bank[use % 2]

            def turn(b, use, xn, xn_ready):
                for k in range(KD):
                    bk = a_take(b, use + k)
                    for j in range(NB):
                        if k == 0:
                            pe.wait_ge(xn_ready, b * NB + j + 1)
                        last = pe.transpose(bk[:, j * P:(j + 1) * P], xn[:, j, k * P:(k + 1) * P], ident[:, :])
                    last.then_inc(a_full, 1)

            def three(out_ap, terms):
                n = len(terms) * 3
                at = 0
                for lh, ll, rh, rl in terms:
                    for l, r in ((lh, rh), (lh, rl), (ll, rh)):
                        last = pe.matmul(out_ap, l, r, start=(at == 0), stop=(at == n - 1))
                        at += 1
                return last

            def z_products(b):
                for m in range(KD):
                    bk = a_take(b, ZT + m, need=XT + KD)
                    ms = slice(m * P, (m + 1) * P)
                    three(bk[:, :], [(m_hi[:, k, ms], m_lo[:, k, ms], xT_hi[:, k, :], xT_lo[:, k, :])
                                     for k in range(KD)]).then_inc(a_full, 1)

            def u_products(b):
                for h in range(2):
                    bk = a_take(b, UV + h)
                    for j in (2 * h, 2 * h + 1):
                        js = slice(j * P, (j + 1) * P)
                        last = three(bk[:, (j % 2) * D:(j % 2 + 1) * D],
                                     [(xT_hi[:, k, js], xT_lo[:, k, js], wvo_hi[:, k, :], wvo_lo[:, k, :])
                                      for k in range(KD)])
                    last.then_inc(a_full, 1)

            def scores(b):
                for h, parts in enumerate(([(0, 0, 0), (1, P, 2 * P)], [(3, 2 * P, 0), (2, 2 * P, 2 * P)])):
                    bk = a_take(b, SC + h, need=ZT + KD)
                    for j, q0, c0 in parts:
                        js, qs = slice(j * P, (j + 1) * P), slice(q0, q0 + 2 * P)
                        last = three(bk[:, c0:c0 + 2 * P],
                                     [(xT_hi[:, k, js], xT_lo[:, k, js], z_hi[:, k, qs], z_lo[:, k, qs])
                                      for k in range(KD)])
                    last.then_inc(a_full, 1)

            AT = {(0, 0): (0, 0), (0, 1): (0, P), (1, 1): (0, 2 * P), (1, 2): (0, 3 * P),
                  (3, 3): (1, P), (2, 2): (1, 2 * P), (2, 3): (1, 3 * P)}

            def attend(b):
                for h in range(2):
                    bk = a_take(b, YA + h, need=UV + 2)
                    pe.wait_ge(at_lo_ready, b * 2 + h + 1)
                    for i in (2 * h, 2 * h + 1):
                        terms = []
                        for j in ([i - 1] if i else []) + [i]:
                            g, c = AT[(j, i)]
                            terms.append((at_hi[:, g, c:c + P], at_lo[:, g, c:c + P], u_hi[:, j, :], u_lo[:, j, :]))
                        last = three(bk[:, (i % 2) * D:(i % 2 + 1) * D], terms)
                    last.then_inc(a_full, 1)

            def up(b, n):
                hc = UP_ORDER[n]
                if n == 0:
                    pe.wait_ge(a_drained, b * A_USES + A_USES)
                if not (isinstance(b, int) and b == 0 and n < 2):
                    pe.wait_ge(hid_ready, b * NU + n - 1)
                chunks = [hc, HC + hc] if hc < HC else [2 * HC]
                for g, c in enumerate(chunks):
                    at = 0
                    for k in range(KD):
                        for part in (x2T_hi, x2T_lo):
                            last = pe.matmul(up_bank[n % 2][g][:, :], w12T[:, k, c, :], part[:, k, :],
                                             start=(at == 0), stop=(at == 2 * KD - 1))
                            at += 1
                last.then_inc(up_full, 1)

            def down(b, n):
                hc = UP_ORDER[n]
                pe.wait_ge(hid_lo_ready, b * NU + n + 1)
                for j in range(NB):
                    if n == 0 and j % 2 == 0 and not (isinstance(b, int) and b == 0):
                        pe.wait_ge(out_ready, b * 2 + j // 2 - 1)
                    js = slice(j * P, (j + 1) * P)
                    parts = [hid_hi[:, hc, js], hid_lo[:, hc, js]] if hc < HC else [tail_st[:, js]]
                    for q, part in enumerate(parts):
                        last = pe.matmul(d_bank[j // 2][:, (j % 2) * D:(j % 2 + 1) * D], part, w3T[:, hc, :],
                                         start=(n == 0 and j % 2 == 0 and q == 0), stop=(n == NU - 1 and q == len(parts) - 1),
                                         skip_group_check=True)
                    if n == NU - 1 and j % 2 == 1:
                        last.then_inc(d_full, 1)

            def turn_ternary(fills):
                for n, blocks in fills:
                    if n >= 4:
                        pe.wait_ge(prep_drained, n - 3)
                    for q, (hi, lo) in enumerate(blocks):
                        o = prep_bank[n % 4][:, q * P:(q + 1) * P]
                        pe.matmul(o, hi, ident_bf[:, :], start=True, stop=False)
                        last = pe.matmul(o, lo, nident_bf[:, :], start=False, stop=True)
                    last.then_inc(prep_full, 1)

            pe.wait_ge(wat_loaded, 16)
            for k in range(KD):
                for c in range(KD):
                    last = pe.matmul(d_bank[0][:, k * D:(k + 1) * D], wat[:, c, k * P:(k + 1) * P], wat[:, KD + c, :],
                                     start=(c == 0), stop=(c == KD - 1))
            last.then_inc(comp_full, 1)
            pe.wait_ge(wo_loaded, 16)
            pe.wait_ge(consts_ready, 1)
            for e in range(KD):
                for c in range(KD):
                    last = pe.transpose(d_bank[1][:, e * D + c * P:e * D + (c + 1) * P], wo_n[:, c, e * P:(e + 1) * P],
                                        ident[:, :])
            last.then_inc(comp_full, 1)
            turn(0, XT, xn1, xn1_ready)
            pe.wait_ge(comp_done, 1)
            pe.wait_ge(wo_turned, 1)
            for k in range(KD):
                for c in range(KD):
                    last = pe.matmul(d_bank[0][:, k * D:(k + 1) * D], wat[:, 2 * KD + c, k * P:(k + 1) * P], woT[:, c, :],
                                     start=(c == 0), stop=(c == KD - 1))
            last.then_inc(comp_full, 1)
            z_products(0)
            pe.wait_ge(comp_done, 2)
            u_products(0)
            pe.wait_ge(part_ready, 5)
            pe.matmul(d_bank[1][:, 0:3 * PS], ones[:, :], abs_part[:, :], start=True, stop=True).then_inc(comp_full, 1)
            scores(0)
            blocks = [(above12[:, c, k * P:(k + 1) * P], below12[:, c, k * P:(k + 1) * P])
                      for k in range(KD) for c in range(NCH)]
            fills12 = [(n, blocks[4 * n:4 * n + 4]) for n in range((len(blocks) + 3) // 4)]
            blocks = [(above3[:, k, c * P:(c + 1) * P], below3[:, k, c * P:(c + 1) * P])
                      for c in range(HC + 1) for k in range(KD)]
            fills3 = [(len(fills12) + n, blocks[4 * n:4 * n + 4]) for n in range(len(blocks) // 4)]
            pe.wait_ge(consts_ready, 3)
            pe.wait_ge(ternary_ready, 6)
            turn_ternary(fills12[:4])
            attend(0)
            turn_ternary(fills12[4:])
            pe.wait_ge(ternary_ready, 10)
            turn_ternary(fills3)
            turn(0, X2T, xn2, xn2_ready)
            pe.wait_ge(prep_drained, len(fills12) + len(fills3))

            def step(a, f):
                turn(a, XT, xn1, xn1_ready)
                up(f, 0)
                z_products(a)
                up(f, 1)
                u_products(a)
                up(f, 2)
                up(f, 3)
                scores(a)
                up(f, 4)
                down(f, 0)
                attend(a)
                down(f, 1)
                up(f, 5)
                down(f, 2)
                down(f, 3)
                down(f, 4)
                turn(a, X2T, xn2, xn2_ready)
                down(f, 5)

            step(1, 0)
            with pe.Fori(2, B) as i:
                step(i, i - 1)
            for n in range(NU):
                up(B - 1, n)
                if n >= 2:
                    down(B - 1, n - 2)
            down(B - 1, NU - 2)
            down(B - 1, NU - 1)

        @block.scalar
        def _(act):
            def high(b, use, dst):
                act.wait_ge(a_full, b * A_USES + use + 1)
                act.activation(dst, a_bank[use % 2][:, :], ACT.Copy).then_inc(a_hi, 1)

            def high_pair(b, use, dst):
                for n in range(2):
                    high(b, use + n, dst(n))

            def x_high(b):
                high_pair(b, XT, lambda k: xT_hi[:, k, :])

            def z_high(b):
                high_pair(b, ZT, lambda m: z_hi[:, m, :])

            def u_high(b):
                high_pair(b, UV, lambda h: u_hi[:, 2 * h:2 * h + 2, :].rearrange("p j d -> p (j d)"))

            def x2_high(b):
                high_pair(b, X2T, lambda k: x2T_hi[:, k, :])

            def squares(b):
                for h in range(2):
                    cols = slice(0, 512) if h == 0 else slice(P, 512)
                    act.wait_ge(a_drained, b * A_USES + SC + h + 1)
                    if not (isinstance(b, int) and b == 0):
                        act.wait_ge(at_lo_ready, b * 2 + h - 1)
                    act.activation(sc_sq[:, h, cols], sc_pos[:, h, cols], ACT.Square, scale=1.0 / WINDOW).then_inc(sq_ready, 1)
                    act.activation(at_hi[:, h, cols], sc_pos[:, h, cols], ACT.Square, scale=1.0 / WINDOW).then_inc(at_hi_ready, 1)

            def gates(b, n):
                hc = UP_ORDER[n]
                act.wait_ge(up_full, b * NU + n + 1)
                if not (isinstance(b, int) and b == 0 and n < 2):
                    act.wait_ge(hid_ready, b * NU + n - 1)
                if hc < HC:
                    g = act.activation(gate[:, n % 2, :], up_bank[n % 2][0][:, :], ACT.Sigmoid)
                else:
                    g = act.activation(gate[0:TAIL, n % 2, :], up_bank[n % 2][0][TAIL:P, :], ACT.Sigmoid)
                g.then_inc(gate_ready, 1)

            def hid_high(b, n):
                hc = UP_ORDER[n]
                act.wait_ge(hid_ready, b * NU + n + 1)
                if hc < HC:
                    act.activation(hid_hi[:, hc, :], hid[:, n % 2, :], ACT.Copy).then_inc(hid_hi_ready, 1)
                else:
                    act.activation(tail_st[TAIL:P, :], hid[0:TAIL, n % 2, :], ACT.Copy).then_inc(hid_hi_ready, 1)
                    act.activation(tail_hi[0:TAIL, :], hid[0:TAIL, n % 2, :], ACT.Copy).then_inc(hid_hi_ready, 1)

            def drain_ternary(ns):
                for n in ns:
                    act.wait_ge(prep_full, n + 1)
                    nb12 = KD * NCH
                    if n < (nb12 + 3) // 4:
                        lo, hi = 4 * n, min(4 * n + 4, nb12)
                        dst = w12T[:, :, :, :].rearrange("p k c q -> p (k c q)")[:, lo * P:hi * P]
                    else:
                        lo = 4 * (n - (nb12 + 3) // 4)
                        hi = lo + 4
                        dst = w3T[:, :, :].rearrange("p c d -> p (c d)")[:, lo * P:hi * P]
                    act.activation(dst, prep_bank[n % 4][:, 0:(hi - lo) * P], ACT.Copy).then_inc(prep_drained, 1)

            act.dma_start(wat[:, :, :], w_attn.rearrange("(c p) d -> p c d", p=P)).then_inc(wat_loaded, 16)
            act.dma_start(wo_n[:, :, :], w_o.rearrange("(c p) d -> p c d", p=P)).then_inc(wo_loaded, 16)
            act.wait_ge(comp_full, 1)
            act.activation(m_hi[:, :, :].rearrange("p k d -> p (k d)"), d_bank[0][:, :], ACT.Copy).then_inc(comp_hi, 1)
            act.wait_ge(comp_full, 2)
            act.activation(woT[:, :, :].rearrange("p k d -> p (k d)"), d_bank[1][:, :], ACT.Copy).then_inc(wo_turned, 1)
            x_high(0)
            act.wait_ge(comp_full, 3)
            act.activation(wvo_hi[:, :, :].rearrange("p k d -> p (k d)"), d_bank[0][:, :], ACT.Copy).then_inc(comp_hi, 1)
            z_high(0)
            u_high(0)
            squares(0)
            drain_ternary(range(9))
            x2_high(0)

            def step(a, f):
                x_high(a)
                gates(f, 0)
                z_high(a)
                hid_high(f, 0)
                gates(f, 1)
                u_high(a)
                hid_high(f, 1)
                gates(f, 2)
                gates(f, 3)
                hid_high(f, 2)
                hid_high(f, 3)
                squares(a)
                gates(f, 4)
                hid_high(f, 4)
                gates(f, 5)
                hid_high(f, 5)
                x2_high(a)

            step(1, 0)
            with act.Fori(2, B) as i:
                step(i, i - 1)
            for n in range(NU):
                gates(B - 1, n)
                if n:
                    hid_high(B - 1, n - 1)
            hid_high(B - 1, NU - 1)

        @block.vector
        def _(dve):
            def moments(b, stats, stats_done, mv, mv_ready):
                for j in range(NB):
                    dve.bn_stats(stats[:, j, :], xblk(b, j)).then_inc(stats_done, 1)
                wait_alone(dve, stats_done, b * NB + NB)
                for j in range(NB):
                    dve.bn_aggr(mv[:, j, :], stats[:, j, :]).then_inc(mv_ready, 1)

            def normalise(b, mv, rstd, rstd_ready, xn, xn_ready):
                dve.wait_ge(rstd_ready, b + 1)
                for j in range(NB):
                    dve.tensor_scalar(xn[:, j, :], xblk(b, j), mv[:, j, 0:1], rstd[:, j:j + 1],
                                      ALU.subtract, ALU.mult).then_inc(xn_ready, 1)

            def low(b, use, hi, dst):
                dve.wait_ge(a_hi, b * 8 + {XT: 0, ZT: 2, UV: 4, X2T: 6}[use - use % 2] + use % 2 + 1)
                dve.tensor_tensor(dst, a_bank[use % 2][:, :], hi.bitcast(F32), ALU.subtract).then_inc(a_drained, 1)

            def x_low(b):
                for k in range(KD):
                    low(b, XT + k, xT_hi[:, k, :], xT_lo[:, k, :])

            def z_low(b):
                for m in range(KD):
                    low(b, ZT + m, z_hi[:, m, :], z_lo[:, m, :])

            def u_low(b):
                for h in range(2):
                    hs = slice(2 * h, 2 * h + 2)
                    low(b, UV + h, u_hi[:, hs, :].rearrange("p j d -> p (j d)"),
                        u_lo[:, hs, :].rearrange("p j d -> p (j d)"))

            def x2_low(b):
                for k in range(KD):
                    low(b, X2T + k, x2T_hi[:, k, :], x2T_lo[:, k, :])

            def mask(b):
                for h in range(2):
                    dve.wait_ge(a_full, b * A_USES + SC + h + 1)
                    if not (isinstance(b, int) and b == 0):
                        dve.wait_ge(at_hi_ready, b * 2 + h - 1)
                    cap = cap01[:, :, :, :].rearrange("p a c q -> p (a c q)") if h == 0 else \
                        cap23[:, :, :].rearrange("p a q -> p (a q)")
                    cols = slice(0, 512) if h == 0 else slice(P, 512)
                    dve.scalar_tensor_tensor(out=sc_pos[:, h, cols], in0=a_bank[h][:, cols], scalar=0.0, in1=cap,
                                             op0=ALU.max, op1=ALU.min).then_inc(a_drained, 1)

            def add_attention(b):
                for h in range(2):
                    dve.wait_ge(a_full, b * A_USES + YA + h + 1)
                    dve.tensor_tensor(xblk(b, 2 * h, 2), a_bank[h][:, :], xblk(b, 2 * h, 2), ALU.add).then_inc(a_drained, 1)
                wait_alone(dve, a_drained, b * A_USES + YA + 2)

            def hidden(b, n):
                hc = UP_ORDER[n]
                dve.wait_ge(gate_ready, b * NU + n + 1)
                if not (isinstance(b, int) and b == 0 and n < 2):
                    dve.wait_ge(hid_lo_ready, b * NU + n - 1)
                rows = slice(0, P) if hc < HC else slice(0, TAIL)
                dve.tensor_tensor(hid[rows, n % 2, :], up_bank[n % 2][1 if hc < HC else 0][rows, :], gate[rows, n % 2, :],
                                  ALU.mult).then_inc(hid_ready, 1)

            def add_ffn(b):
                for h in range(2):
                    dve.wait_ge(d_full, b * 2 + h + 1)
                    dve.tensor_tensor(xblk(b, 2 * h, 2), d_bank[h][:, :], xblk(b, 2 * h, 2), ALU.add).then_inc(out_ready, 1)

            def abs_sum(col, src):
                n = 1
                for s in src.shape[1:]:
                    n *= s
                if len(src.shape) == 3:
                    v = src.rearrange("p c (r e) -> p c r e", e=RED)
                    o = abs_part[:, col:col + n // RED].rearrange("p (c r) -> p c r", c=src.shape[1])
                    return v, o
                return src.rearrange("p (r e) -> p r e", e=RED), None

            dve.memset(abs_part[:, :], 0.0).then_inc(part_zeroed, 1)
            dve.wait_ge(x_loaded, 16)
            moments(0, stats1, stats1_done, mv1, mv1_ready)
            normalise(0, mv1, rstd1, rstd1_ready, xn1, xn1_ready)
            dve.wait_ge(comp_hi, 1)
            dve.tensor_tensor(m_lo[:, :, :].rearrange("p k d -> p (k d)"), d_bank[0][:, :],
                              m_hi[:, :, :].rearrange("p k d -> p (k d)").bitcast(F32), ALU.subtract).then_inc(comp_done, 1)
            x_low(0)
            dve.wait_ge(comp_hi, 2)
            dve.tensor_tensor(wvo_lo[:, :, :].rearrange("p k d -> p (k d)"), d_bank[0][:, :],
                              wvo_hi[:, :, :].rearrange("p k d -> p (k d)").bitcast(F32), ALU.subtract).then_inc(comp_done, 1)
            z_low(0)
            dve.wait_ge(part_zeroed, 1)
            NR = D // RED
            w12_r = w12_n[:, :, :].rearrange("p c (r e) -> p (c r) e", e=RED)
            w3_r = w3_n[:, :, :].rearrange("p c (r e) -> p (c r) e", e=RED)

            def abs_run(o, i):
                dve.tensor_reduce(o, i, AX_X, ALU.add, apply_absolute_value=True).then_inc(part_ready, 1)

            dve.wait_ge(w1_loaded, 32)
            abs_run(abs_part[:, 0:HC * NR], w12_r[:, 0:HC * NR, :])
            abs_run(abs_part[TAIL:P, HC * NR:HC * NR + NR], w12_r[TAIL:P, 2 * HC * NR:NCH * NR, :])
            dve.wait_ge(w2_loaded, 32)
            abs_run(abs_part[:, PS:PS + HC * NR], w12_r[:, HC * NR:2 * HC * NR, :])
            abs_run(abs_part[0:TAIL, PS + HC * NR:PS + HC * NR + NR], w12_r[0:TAIL, 2 * HC * NR:NCH * NR, :])
            dve.wait_ge(w3_loaded, 16)
            abs_run(abs_part[:, 2 * PS:2 * PS + KD * H // RED], w3_r[:, :, :])
            u_low(0)
            dve.wait_ge(comp_full, 4)
            dve.tensor_reduce(abs_total[:, :], d_bank[1][:, 0:3 * PS].rearrange("p (w c) -> p w c", w=3), AX_X,
                              ALU.add).then_inc(total_ready, 1)
            dve.wait_ge(caps_ready, 4)
            mask(0)
            dve.wait_ge(total_ready, 1)
            half_mean, half_eps = 0.5 / (H * D), 0.5 * QUANT_EPS
            for t, sign in ((thr, 1.0), (nthr, -1.0)):
                dve.tensor_scalar(t[:, 0:3], abs_total[:, :], sign * half_mean, sign * half_eps, ALU.mult, ALU.add)\
                   .then_inc(thr_ready, 1)
                for rows, c in ((slice(TAIL, P), 0), (slice(0, TAIL), 1)):
                    dve.tensor_scalar(t[rows, 3:4], abs_total[rows, c:c + 1], sign * half_mean, sign * half_eps,
                                      ALU.mult, ALU.add).then_inc(thr_ready, 1)
            dve.wait_ge(thr_ready, 6)

            def ternary(above, below, src, c):
                dve.tensor_scalar(above, src, thr[:, c:c + 1], None, ALU.is_gt).then_inc(ternary_ready, 1)
                dve.tensor_scalar(below, src, nthr[:, c:c + 1], None, ALU.is_lt).then_inc(ternary_ready, 1)

            ternary(above12[:, 0:HC, :], below12[:, 0:HC, :], w12_n[:, 0:HC, :], 0)
            ternary(above12[:, HC:2 * HC, :], below12[:, HC:2 * HC, :], w12_n[:, HC:2 * HC, :], 1)
            ternary(above12[:, 2 * HC, :], below12[:, 2 * HC, :], w12_n[:, 2 * HC, :], 3)
            add_attention(0)
            moments(0, stats2, stats2_done, mv2, mv2_ready)
            ternary(above3[:, :, 0:H], below3[:, :, 0:H], w3_n[:, :, :], 2)
            ternary(above3[:, :, H:H3], below3[:, :, H:H3], w3_n[:, :, HC * P:H], 2)
            normalise(0, mv2, rstd2, rstd2_ready, xn2, xn2_ready)
            dve.wait_ge(x_loaded, 32)
            moments(1, stats1, stats1_done, mv1, mv1_ready)
            normalise(1, mv1, rstd1, rstd1_ready, xn1, xn1_ready)
            x2_low(0)

            def step(a, f, ahead):
                x_low(a)
                hidden(f, 0)
                z_low(a)
                hidden(f, 1)
                u_low(a)
                hidden(f, 2)
                hidden(f, 3)
                mask(a)
                if ahead:
                    wait_alone(dve, x_loaded, 16 * a + 32)
                    moments(a + 1, stats1, stats1_done, mv1, mv1_ready)
                hidden(f, 4)
                if ahead:
                    normalise(a + 1, mv1, rstd1, rstd1_ready, xn1, xn1_ready)
                add_attention(a)
                moments(a, stats2, stats2_done, mv2, mv2_ready)
                hidden(f, 5)
                normalise(a, mv2, rstd2, rstd2_ready, xn2, xn2_ready)
                x2_low(a)
                add_ffn(f)

            step(1, 0, True)
            with dve.Fori(2, B - 1) as i:
                step(i, i - 1, True)
            step(B - 1, B - 2, False)
            for n in range(NU):
                hidden(B - 1, n)
            add_ffn(B - 1)

        @block.gpsimd
        def _(pool):
            def inv_std(b, mv, mv_ready, veps, veps_ready, rstd, rstd_ready):
                wait_alone(pool, mv_ready, b * NB + NB)
                pool.tensor_scalar(veps[:, :], mv[:, :, 1], LN_EPS, None, ALU.add).then_inc(veps_ready, 1)
                pool.wait_ge(veps_ready, b + 1)
                pool.tensor_tensor(rstd[:, :], veps[:, :], neg_half[:, :], ALU.pow).then_inc(rstd_ready, 1)

            def inv_std1(b):
                inv_std(b, mv1, mv1_ready, veps1, veps1_ready, rstd1, rstd1_ready)

            def inv_std2(b):
                inv_std(b, mv2, mv2_ready, veps2, veps2_ready, rstd2, rstd2_ready)

            def hid_low(b, n):
                hc = UP_ORDER[n]
                pool.wait_ge(hid_hi_ready, b * (NU + 1) + n + 1 + (n >= UP_ORDER.index(HC)))
                if hc < HC:
                    o, i, h = hid_lo[:, hc, :], hid[:, n % 2, :], hid_hi[:, hc, :]
                else:
                    o, i, h = tail_st[0:TAIL, :], hid[0:TAIL, n % 2, :], tail_hi[0:TAIL, :]
                pool.tensor_tensor(o, i, h.bitcast(F32), ALU.subtract).then_inc(hid_lo_ready, 1)

            def at_low(b):
                for h in range(2):
                    cols = slice(0, 512) if h == 0 else slice(P, 512)
                    pool.wait_ge(sq_ready, b * 2 + h + 1)
                    pool.wait_ge(at_hi_ready, b * 2 + h + 1)
                    pool.tensor_tensor(at_lo[:, h, cols], sc_sq[:, h, cols], at_hi[:, h, cols].bitcast(F32),
                                       ALU.subtract).then_inc(at_lo_ready, 1)

            pool.memset(ident[:, :], 0.0).then_inc(zeroed, 1)
            pool.memset(neg_half[:, :], -0.5).then_inc(zeroed, 1)
            pool.memset(ones[:, :], 1.0).then_inc(zeroed, 1)
            pool.wait_ge(zeroed, 3)
            pool.affine_select(out=ident[:, :], in_=ident[:, :], compare_op=ALU.not_equal, fill=1.0, base=0,
                               pattern=[[-1, P]], channel_multiplier=1).then_inc(consts_ready, 1)
            inv_std1(0)
            pool.memset(cap01[:, :, :, :], BIG).then_inc(zeroed, 1)
            pool.memset(cap23[:, :, :], BIG).then_inc(zeroed, 1)
            pool.wait_ge(zeroed, 5)
            same = dict(compare_op=ALU.is_ge, fill=0.0, base=0, channel_multiplier=-1)
            before = dict(compare_op=ALU.is_ge, fill=0.0, base=0, channel_multiplier=1)
            pool.affine_select(out=cap01[:, :, 0, :], in_=cap01[:, :, 0, :], pattern=[[0, 2], [1, P]], **same).then_inc(caps_ready, 1)
            pool.affine_select(out=cap01[:, :, 1, :], in_=cap01[:, :, 1, :], pattern=[[0, 2], [-1, P]], **before).then_inc(caps_ready, 1)
            pool.affine_select(out=cap23[:, 0:2, :], in_=cap23[:, 0:2, :], pattern=[[0, 2], [1, P]], **same).then_inc(caps_ready, 1)
            pool.affine_select(out=cap23[:, 2, :], in_=cap23[:, 2, :], pattern=[[-1, P]], **before).then_inc(caps_ready, 1)
            pool.wait_ge(consts_ready, 1)
            pool.tensor_copy(ident_bf[:, :], ident[:, :]).then_inc(consts_ready, 1)
            pool.tensor_scalar(nident_bf[:, :], ident[:, :], -1.0, None, ALU.mult).then_inc(consts_ready, 1)
            at_low(0)
            inv_std2(0)
            inv_std1(1)

            def step(a, f, ahead):
                for n in range(4):
                    hid_low(f, n)
                at_low(a)
                if ahead:
                    inv_std1(a + 1)
                hid_low(f, 4)
                inv_std2(a)
                hid_low(f, 5)

            step(1, 0, True)
            with pool.Fori(2, B - 1) as i:
                step(i, i - 1, True)
            step(B - 1, B - 2, False)
            for n in range(NU):
                hid_low(B - 1, n)


_INS = ['L0_attn_x', 'L0_attn_w_attn', 'L0_attn_w_o', 'L0_ffn_w1', 'L0_ffn_w2', 'L0_ffn_w3']


def kernel(**inputs):
    import numpy as _np
    import concourse.bacc as _bacc
    from concourse import mybir as _mybir
    from concourse.bass_utils import run_bass_kernel_spmd as _run

    nc = _bacc.Bacc("TRN2", target_bir_lowering=False, num_devices=1)
    arrays, args = {}, []
    for name in _INS:
        a = _np.ascontiguousarray(inputs[name])
        arrays[f"in_{name}_dram"] = a
        args.append(nc.dram_tensor(f"in_{name}_dram", a.shape, _mybir.dt.from_np(a.dtype), kind="ExternalInput").ap())
    shape = inputs['L0_attn_x'].shape
    args.append(nc.dram_tensor("out_0_dram", shape, _mybir.dt.float32, kind="ExternalOutput").ap())
    build(nc, *args)
    r = _run(nc, [arrays], core_ids=[0])
    return r.results[0]["out_0_dram"]
```

```python
from contextlib import ExitStack

import concourse.bass as bass
from concourse import mybir

P = 128
F32 = mybir.dt.float32
F32R = mybir.dt.float32r
BF16 = mybir.dt.bfloat16
ALU = mybir.AluOpType
ACT = mybir.ActivationFunctionType
AX_X = mybir.AxisListType.X

LN_EPS = 1e-5
QUANT_EPS = 1e-8
BIG = 3.4028234663852886e38

ZT, UV, SC, YA, XT, X2T = range(6)
A_USES = 12
FIRST_TURNS = {(0, XT): 0, (0, ZT): 2, (0, SC): 4, (0, UV): 6, (1, XT): 8, (0, YA): 10, (1, ZT): 12, (1, UV): 14,
               (0, X2T): 16}
FIRST_HIGHS = {(0, XT): 0, (0, ZT): 2, (0, UV): 4, (1, XT): 6, (1, ZT): 8, (1, UV): 10, (0, X2T): 12}


def turn_of(b, stage, last):
    if isinstance(b, int) and (b, stage) in FIRST_TURNS:
        return FIRST_TURNS[b, stage]
    if stage == XT:
        return b * A_USES - 2
    if stage == X2T:
        return b * A_USES + (10 if isinstance(b, int) and b == last else 12)
    return b * A_USES + 2 + 2 * stage


def highs_of(b, stage, last):
    if isinstance(b, int) and (b, stage) in FIRST_HIGHS:
        return FIRST_HIGHS[b, stage]
    if stage == XT:
        return b * 8 - 2
    if stage == X2T:
        return b * 8 + (6 if isinstance(b, int) and b == last else 8)
    return b * 8 + 2 + 2 * stage


def build(nc, x, w_attn, w_o, w1, w2, w3, out):
    B, T, D = x.shape
    H = w1.shape[0]
    NB = T // P
    KD = D // P
    HC = H // P
    TAIL = H - HC * P
    assert NB == 4 and KD == 2 and TAIL == 64 and T == 512
    XB = NB * D
    NCH = 2 * HC + 1
    NU = HC + 1
    PS = 2
    WINDOW = float(P)

    x_dram = x.rearrange("b (j p) d -> p b j d", p=P)
    out_dram = out.rearrange("b (j p) d -> p b j d", p=P)

    with ExitStack() as ctx:
        def sb(name, shape, dt=F32):
            return ctx.enter_context(nc.sbuf_tensor(name, shape, dt))

        def bank(name):
            return ctx.enter_context(nc.psum_tensor(name, [P, 512], F32))

        def sem(name):
            return ctx.enter_context(nc.semaphore(name))

        xs = sb("xs", [P, B * XB])
        wat = sb("wat", [P, 3 * KD, D])
        wo_n = sb("wo_n", [P, KD, D])
        woT = sb("woT", [P, KD, D])
        w12_n = sb("w12_n", [P, NCH, D])
        w3_n = sb("w3_n", [P, KD, H])
        m_hi, m_lo = sb("m_hi", [P, KD, D], F32R), sb("m_lo", [P, KD, D], F32R)
        wvo_hi, wvo_lo = sb("wvo_hi", [P, KD, D], F32R), sb("wvo_lo", [P, KD, D], F32R)
        above12, below12 = sb("above12", [P, NCH, D], BF16), sb("below12", [P, NCH, D], BF16)
        H3 = (HC + 1) * P
        above3, below3 = sb("above3", [P, KD, H3], BF16), sb("below3", [P, KD, H3], BF16)
        w12T = sb("w12T", [P, KD, NCH, P], F32R)
        w3T = sb("w3T", [P, HC + 1, D], F32R)
        abs_part = sb("abs_part", [P, 3 * PS])
        abs_total = sb("abs_total", [P, 3])
        thr, nthr = sb("thr", [P, 4]), sb("nthr", [P, 4])
        ident = sb("ident", [P, P])
        ident_bf, nident_bf = sb("ident_bf", [P, P], BF16), sb("nident_bf", [P, P], BF16)
        ones = sb("ones", [P, P])
        neg_half = sb("neg_half", [P, NB])
        cap01 = sb("cap01", [P, 2, 2, P])
        cap23 = sb("cap23", [P, 3, P])

        stats1, stats2 = sb("stats1", [P, NB, 6]), sb("stats2", [P, NB, 6])
        mv1, mv2 = sb("mv1", [P, NB, 2]), sb("mv2", [P, NB, 2])
        veps1, veps2 = sb("veps1", [P, NB]), sb("veps2", [P, NB])
        rstd1, rstd2 = sb("rstd1", [P, NB]), sb("rstd2", [P, NB])
        xn1, xn2 = sb("xn1", [P, NB, D]), sb("xn2", [P, NB, D])
        xT_hi, xT_lo = sb("xT_hi", [P, KD, T], F32R), sb("xT_lo", [P, KD, T], F32R)
        x2T_hi, x2T_lo = sb("x2T_hi", [P, KD, T], F32R), sb("x2T_lo", [P, KD, T], F32R)
        z_hi, z_lo = sb("z_hi", [P, KD, T], F32R), sb("z_lo", [P, KD, T], F32R)
        u_hi, u_lo = sb("u_hi", [P, NB, D], F32R), sb("u_lo", [P, NB, D], F32R)
        sc_pos = sb("sc_pos", [P, 2, 512])
        sc_sq = sb("sc_sq", [P, 2, 512])
        at_hi, at_lo = sb("at_hi", [P, 2, 512], F32R), sb("at_lo", [P, 2, 512], F32R)
        gate = sb("gate", [P, 2, T])
        hid = sb("hid", [P, 2, T])
        hid_hi, hid_lo = sb("hid_hi", [P, HC, T], F32R), sb("hid_lo", [P, HC, T], F32R)
        tail_hi = sb("tail_hi", [TAIL, T], F32R)
        tail_st = sb("tail_st", [P, T], F32R)

        a_bank = [bank("a_bank0"), bank("a_bank1")]
        up_bank = [[bank(f"up{r}_{g}") for g in range(2)] for r in range(2)]
        d_bank = [bank("d_bank0"), bank("d_bank1")]
        prep_bank = [up_bank[0][0], up_bank[0][1], up_bank[1][0], up_bank[1][1]]

        x_loaded = sem("x_loaded")
        wat_loaded, wo_loaded, wv_loaded = sem("wat_loaded"), sem("wo_loaded"), sem("wv_loaded")
        w1_loaded, w2_loaded, w3_loaded = sem("w1_loaded"), sem("w2_loaded"), sem("w3_loaded")
        zeroed, consts_ready, caps_ready = sem("zeroed"), sem("consts_ready"), sem("caps_ready")
        comp_full = sem("comp_full")
        comp_hi, comp_done = sem("comp_hi"), sem("comp_done")
        wo_turned = sem("wo_turned")
        part_zeroed, part_ready = sem("part_zeroed"), sem("part_ready")
        total_ready, thr_ready = sem("total_ready"), sem("thr_ready")
        ternary_ready, below3_ready = sem("ternary_ready"), sem("below3_ready")
        prep_full, prep_drained = sem("prep_full"), sem("prep_drained")
        stats1_done, mv1_ready, veps1_ready, rstd1_ready, xn1_ready = (
            sem("stats1_done"), sem("mv1_ready"), sem("veps1_ready"), sem("rstd1_ready"), sem("xn1_ready"))
        stats2_done, mv2_ready, veps2_ready, rstd2_ready, xn2_ready = (
            sem("stats2_done"), sem("mv2_ready"), sem("veps2_ready"), sem("rstd2_ready"), sem("xn2_ready"))
        a_full = sem("a_full")
        a_hi = sem("a_hi")
        a_drained = sem("a_drained")
        sq_ready, at_hi_ready, at_lo_ready = sem("sq_ready"), sem("at_hi_ready"), sem("at_lo_ready")
        up_full, gate_ready = sem("up_full"), sem("gate_ready")
        hid_ready = sem("hid_ready")
        hid_hi_ready, hid_lo_ready, hid_lo_last = sem("hid_hi_ready"), sem("hid_lo_ready"), sem("hid_lo_last")
        d_full, out_ready = sem("d_full"), sem("out_ready")
        stored = sem("stored")
        waits_alone = sem("waits_alone")

        block = ctx.enter_context(nc.Block())

        def wait_alone(eng, what, count):
            eng.wait_ge(what, count)
            eng.sem_inc(waits_alone, 1)

        def low_of(n):
            if n < HC:
                return hid_lo[:, n, :], hid[:, n % 2, :], hid_hi[:, n, :]
            return tail_st[0:TAIL, :], hid[0:TAIL, n % 2, :], tail_hi[0:TAIL, :]

        def xblk(b, j, n=1):
            return xs[:, bass.ds(b * XB + j * D, n * D)]

        @block.sync
        def _(sp):
            sp.dma_start(xblk(0, 0, NB).rearrange("p (j d) -> p j d", j=NB), x_dram[:, 0]).then_inc(x_loaded, 16)
            sp.dma_start(w12_n[:, 0:HC, :], w1[0:HC * P, :].rearrange("(c p) d -> p c d", p=P)).then_inc(w1_loaded, 16)
            sp.dma_start(w12_n[TAIL:P, 2 * HC, :], w1[HC * P:H, :]).then_inc(w1_loaded, 16)
            sp.wait_ge(x_loaded, 16)
            sp.dma_start(xblk(1, 0, NB).rearrange("p (j d) -> p j d", j=NB), x_dram[:, 1]).then_inc(x_loaded, 16)
            sp.dma_start(w12_n[:, HC:2 * HC, :], w2[0:HC * P, :].rearrange("(c p) d -> p c d", p=P)).then_inc(w2_loaded, 16)
            sp.dma_start(w12_n[0:TAIL, 2 * HC, :], w2[HC * P:H, :]).then_inc(w2_loaded, 16)
            sp.dma_start(w3_n[:, :, :], w3.rearrange("(c p) h -> p c h", p=P)).then_inc(w3_loaded, 16)
            with sp.Fori(2, B) as i:
                sp.wait_ge(x_loaded, 16 * i)
                dst = xs[:, bass.ds(i * XB, XB)].rearrange("p (j d) -> p j d", j=NB)
                src = x_dram[:, bass.ds(i, 1)].rearrange("p o j d -> p (o j) d")
                sp.dma_start(dst, src).then_inc(x_loaded, 16)
            with sp.Fori(0, B) as i:
                sp.wait_ge(out_ready, 2 * i + 2)
                dst = out_dram[:, bass.ds(i, 1)].rearrange("p o j d -> p (o j) d")
                src = xs[:, bass.ds(i * XB, XB)].rearrange("p (j d) -> p j d", j=NB)
                sp.dma_start(dst, src).then_inc(stored, 16)
            sp.wait_ge(stored, 16 * B)

        @block.tensor
        def _(pe):
            def a_take(b, stage, h, need=None):
                drained = turn_of(b, stage, B - 1) + h - 1
                if need is not None:
                    b0 = b if isinstance(b, int) else 3
                    if turn_of(b0, need, B - 1) + 2 > turn_of(b0, stage, B - 1) + h - 1:
                        drained = turn_of(b, need, B - 1) + 2
                if not (isinstance(drained, int) and drained <= 0):
                    pe.wait_ge(a_drained, drained)
                return a_bank[h]

            def turn(b, stage, xn, xn_ready):
                for k in range(KD):
                    bk = a_take(b, stage, k)
                    for j in range(NB):
                        if k == 0:
                            pe.wait_ge(xn_ready, b * NB + j + 1)
                        last = pe.transpose(bk[:, j * P:(j + 1) * P], xn[:, j, k * P:(k + 1) * P], ident[:, :])
                    last.then_inc(a_full, 1)

            def three(out_ap, terms):
                n = len(terms) * 3
                at = 0
                for lh, ll, rh, rl in terms:
                    for l, r in ((lh, rh), (lh, rl), (ll, rh)):
                        last = pe.matmul(out_ap, l, r, start=(at == 0), stop=(at == n - 1))
                        at += 1
                return last

            def z_products(b):
                for m in range(KD):
                    bk = a_take(b, ZT, m, need=XT)
                    ms = slice(m * P, (m + 1) * P)
                    three(bk[:, :], [(m_hi[:, k, ms], m_lo[:, k, ms], xT_hi[:, k, :], xT_lo[:, k, :])
                                     for k in range(KD)]).then_inc(a_full, 1)

            def u_products(b):
                for h in range(2):
                    bk = a_take(b, UV, h)
                    for j in (2 * h, 2 * h + 1):
                        js = slice(j * P, (j + 1) * P)
                        last = three(bk[:, (j % 2) * D:(j % 2 + 1) * D],
                                     [(xT_hi[:, k, js], xT_lo[:, k, js], wvo_hi[:, k, :], wvo_lo[:, k, :])
                                      for k in range(KD)])
                    last.then_inc(a_full, 1)

            def scores(b):
                for h, parts in enumerate(([(0, 0, 0), (1, P, 2 * P)], [(3, 2 * P, 0), (2, 2 * P, 2 * P)])):
                    bk = a_take(b, SC, h, need=ZT)
                    for j, q0, c0 in parts:
                        js, qs = slice(j * P, (j + 1) * P), slice(q0, q0 + 2 * P)
                        last = three(bk[:, c0:c0 + 2 * P],
                                     [(xT_hi[:, k, js], xT_lo[:, k, js], z_hi[:, k, qs], z_lo[:, k, qs])
                                      for k in range(KD)])
                    last.then_inc(a_full, 1)

            AT = {(0, 0): (0, 0), (0, 1): (0, P), (1, 1): (0, 2 * P), (1, 2): (0, 3 * P),
                  (3, 3): (1, P), (2, 2): (1, 2 * P), (2, 3): (1, 3 * P)}

            def attend(b):
                for h in range(2):
                    bk = a_take(b, YA, h, need=UV)
                    pe.wait_ge(at_lo_ready, b * 2 + h + 1)
                    for i in (2 * h, 2 * h + 1):
                        terms = []
                        for j in ([i - 1] if i else []) + [i]:
                            g, c = AT[(j, i)]
                            terms.append((at_hi[:, g, c:c + P], at_lo[:, g, c:c + P], u_hi[:, j, :], u_lo[:, j, :]))
                        last = three(bk[:, (i % 2) * D:(i % 2 + 1) * D], terms)
                    last.then_inc(a_full, 1)

            def up(b, n):
                if n == 0:
                    pe.wait_ge(a_drained, turn_of(b, X2T, B - 1) + 2)
                if not (isinstance(b, int) and b == 0 and n < 2):
                    pe.wait_ge(hid_ready, b * NU + n - 1)
                chunks = [n, HC + n] if n < HC else [2 * HC]
                for g, c in enumerate(chunks):
                    at = 0
                    for k in range(KD):
                        for part in (x2T_hi, x2T_lo):
                            last = pe.matmul(up_bank[n % 2][g][:, :], w12T[:, k, c, :], part[:, k, :],
                                             start=(at == 0), stop=(at == 2 * KD - 1))
                            at += 1
                last.then_inc(up_full, 1)

            def down(b, n, tokens=range(NB)):
                if isinstance(b, int) and b == B - 1 and n >= NU - 2:
                    pe.wait_ge(hid_lo_last, n - (NU - 2) + 1)
                else:
                    pe.wait_ge(hid_lo_ready, b * NU + n + 1)
                if n == HC:
                    pe.wait_ge(hid_hi_ready, b * (NU + 1) + NU + 1)
                for j in tokens:
                    if n == 0 and j % 2 == 0 and not (isinstance(b, int) and b == 0):
                        pe.wait_ge(out_ready, b * 2 + j // 2 - 1)
                    js = slice(j * P, (j + 1) * P)
                    parts = [hid_hi[:, n, js], hid_lo[:, n, js]] if n < HC else [tail_st[:, js]]
                    for q, part in enumerate(parts):
                        last = pe.matmul(d_bank[j // 2][:, (j % 2) * D:(j % 2 + 1) * D], part, w3T[:, n, :],
                                         start=(n == 0 and j % 2 == 0 and q == 0), stop=(n == NU - 1 and q == len(parts) - 1),
                                         skip_group_check=True)
                    if n == NU - 1 and j % 2 == 1:
                        last.then_inc(d_full, 1)

            def turn_ternary(fills):
                for n, blocks in fills:
                    if n >= 4:
                        pe.wait_ge(prep_drained, n - 3)
                    for q, (hi, lo) in enumerate(blocks):
                        o = prep_bank[n % 4][:, q * P:(q + 1) * P]
                        pe.matmul(o, hi, ident_bf[:, :], start=True, stop=False)
                        last = pe.matmul(o, lo, nident_bf[:, :], start=False, stop=True)
                    last.then_inc(prep_full, 1)

            def compose(bk, lhs, rhs):
                for k in range(KD):
                    for c in range(KD):
                        last = pe.matmul(bk[:, k * D:(k + 1) * D], lhs(c)[:, k * P:(k + 1) * P], rhs(c),
                                         start=(c == 0), stop=(c == KD - 1))
                last.then_inc(comp_full, 1)

            blocks = [(above12[:, c, k * P:(k + 1) * P], below12[:, c, k * P:(k + 1) * P])
                      for k in range(KD) for c in range(NCH)]
            fills12 = [(n, blocks[4 * n:4 * n + 4]) for n in range((len(blocks) + 3) // 4)]
            blocks = [(above3[:, k, c * P:(c + 1) * P], below3[:, k, c * P:(c + 1) * P])
                      for c in range(HC + 1) for k in range(KD)]
            fills3 = [(len(fills12) + n, blocks[4 * n:4 * n + 4]) for n in range(len(blocks) // 4)]

            pe.wait_ge(wat_loaded, 16)
            compose(d_bank[0], lambda c: wat[:, c, :], lambda c: wat[:, KD + c, :])
            pe.wait_ge(consts_ready, 1)
            turn(0, XT, xn1, xn1_ready)
            pe.wait_ge(wo_loaded, 16)
            for e in range(KD):
                for c in range(KD):
                    last = pe.transpose(d_bank[1][:, e * D + c * P:e * D + (c + 1) * P], wo_n[:, c, e * P:(e + 1) * P],
                                        ident[:, :])
            last.then_inc(comp_full, 1)
            pe.wait_ge(comp_done, 1)
            z_products(0)
            pe.wait_ge(wo_turned, 1)
            pe.wait_ge(wv_loaded, 16)
            compose(d_bank[0], lambda c: wat[:, 2 * KD + c, :], lambda c: woT[:, c, :])
            scores(0)
            pe.wait_ge(comp_done, 2)
            u_products(0)
            pe.wait_ge(part_ready, 6)
            pe.matmul(d_bank[1][:, 0:3 * PS], ones[:, :], abs_part[:, :], start=True, stop=True).then_inc(comp_full, 1)
            turn(1, XT, xn1, xn1_ready)
            attend(0)
            z_products(1)
            u_products(1)
            pe.wait_ge(consts_ready, 3)
            pe.wait_ge(ternary_ready, 4)
            turn_ternary(fills12[:2])
            pe.wait_ge(ternary_ready, 6)
            turn_ternary(fills12[2:4])
            turn(0, X2T, xn2, xn2_ready)
            turn_ternary(fills12[4:])
            pe.wait_ge(ternary_ready, 8)
            pe.wait_ge(below3_ready, 2)
            turn_ternary(fills3)
            pe.wait_ge(prep_drained, len(fills12) + len(fills3))

            def step(a, f, ahead, begun=False):
                if not begun:
                    z_products(a)
                up(f, 0)
                if not begun:
                    u_products(a)
                up(f, 1)
                up(f, 2)
                scores(a)
                up(f, 3)
                up(f, 4)
                attend(a)
                down(f, 0)
                up(f, 5)
                if ahead:
                    turn(a + 1, XT, xn1, xn1_ready)
                down(f, 1)
                down(f, 2)
                down(f, 3)
                turn(a, X2T, xn2, xn2_ready)
                down(f, 4)
                down(f, 5)

            step(1, 0, True, begun=True)
            with pe.Fori(2, B - 1) as i:
                step(i, i - 1, True)
            step(B - 1, B - 2, False)
            last = B - 1
            for n in (0, 1, 2):
                up(last, n)
            down(last, 0)
            for n in (3, 4, 5):
                up(last, n)
            down(last, 1)
            down(last, 2)
            for tokens in ((0, 1), (2, 3)):
                for n in (3, 4, 5):
                    down(last, n, tokens)

        @block.scalar
        def _(act):
            def high_pair(b, stage, dst, halves=range(2)):
                for h in halves:
                    act.wait_ge(a_full, turn_of(b, stage, B - 1) + h + 1)
                    act.activation(dst(h), a_bank[h][:, :], ACT.Copy).then_inc(a_hi, 1)

            def x_high(b):
                high_pair(b, XT, lambda k: xT_hi[:, k, :])

            def z_high(b):
                high_pair(b, ZT, lambda m: z_hi[:, m, :])

            def u_high(b, halves=range(2)):
                high_pair(b, UV, lambda h: u_hi[:, 2 * h:2 * h + 2, :].rearrange("p j d -> p (j d)"), halves)

            def x2_high(b):
                high_pair(b, X2T, lambda k: x2T_hi[:, k, :])

            def squares(b, h):
                cols = slice(0, 512) if h == 0 else slice(P, 512)
                act.wait_ge(a_drained, turn_of(b, SC, B - 1) + h + 1)
                if not (isinstance(b, int) and b == 0):
                    act.wait_ge(at_lo_ready, b * 2 + h - 1)
                act.activation(sc_sq[:, h, cols], sc_pos[:, h, cols], ACT.Square, scale=1.0 / WINDOW).then_inc(sq_ready, 1)
                act.activation(at_hi[:, h, cols], sc_pos[:, h, cols], ACT.Square, scale=1.0 / WINDOW).then_inc(at_hi_ready, 1)

            def gates(b, n):
                act.wait_ge(up_full, b * NU + n + 1)
                if not (isinstance(b, int) and b == 0 and n < 2):
                    act.wait_ge(hid_ready, b * NU + n - 1)
                if n < HC:
                    g = act.activation(gate[:, n % 2, :], up_bank[n % 2][0][:, :], ACT.Sigmoid)
                else:
                    g = act.activation(gate[0:TAIL, n % 2, :], up_bank[n % 2][0][TAIL:P, :], ACT.Sigmoid)
                g.then_inc(gate_ready, 1)

            def hid_high(b, n):
                act.wait_ge(hid_ready, b * NU + n + 1)
                if n < HC:
                    act.activation(hid_hi[:, n, :], hid[:, n % 2, :], ACT.Copy).then_inc(hid_hi_ready, 1)
                else:
                    act.activation(tail_hi[0:TAIL, :], hid[0:TAIL, n % 2, :], ACT.Copy).then_inc(hid_hi_ready, 1)

            def tail_stack(b):
                act.activation(tail_st[TAIL:P, :], hid[0:TAIL, HC % 2, :], ACT.Copy).then_inc(hid_hi_ready, 1)

            def drain_ternary(ns):
                for n in ns:
                    act.wait_ge(prep_full, n + 1)
                    nb12 = KD * NCH
                    if n < (nb12 + 3) // 4:
                        lo, hi = 4 * n, min(4 * n + 4, nb12)
                        dst = w12T[:, :, :, :].rearrange("p k c q -> p (k c q)")[:, lo * P:hi * P]
                    else:
                        lo = 4 * (n - (nb12 + 3) // 4)
                        hi = lo + 4
                        dst = w3T[:, :, :].rearrange("p c d -> p (c d)")[:, lo * P:hi * P]
                    act.activation(dst, prep_bank[n % 4][:, 0:(hi - lo) * P], ACT.Copy).then_inc(prep_drained, 1)

            def abs_sums(col, c0, rows):
                flat = w12_n[:, :, :].rearrange("p c d -> p (c d)")
                for at, c, n, rs in ((0, c0, HC, slice(0, P)), (1, 2 * HC, 1, rows)):
                    act.activation(above12[rs, c:c + n, :].rearrange("p c d -> p (c d)"), flat[rs, c * D:(c + n) * D], ACT.Abs,
                                   accum_out=abs_part[rs, col + at:col + at + 1]).then_inc(part_ready, 1)

            act.dma_start(wat[:, 0:2 * KD, :], w_attn[0:2 * D, :].rearrange("(c p) d -> p c d", p=P)).then_inc(wat_loaded, 16)
            act.dma_start(wo_n[:, :, :], w_o.rearrange("(c p) d -> p c d", p=P)).then_inc(wo_loaded, 16)
            act.dma_start(wat[:, 2 * KD:3 * KD, :], w_attn[2 * D:3 * D, :].rearrange("(c p) d -> p c d", p=P))\
               .then_inc(wv_loaded, 16)
            act.wait_ge(comp_full, 1)
            act.activation(m_hi[:, :, :].rearrange("p k d -> p (k d)"), d_bank[0][:, :], ACT.Copy).then_inc(comp_hi, 1)
            x_high(0)
            act.wait_ge(comp_full, 2)
            act.activation(woT[:, :, :].rearrange("p k d -> p (k d)"), d_bank[1][:, :], ACT.Copy).then_inc(wo_turned, 1)
            act.wait_ge(part_zeroed, 1)
            act.wait_ge(w1_loaded, 32)
            abs_sums(0, 0, slice(TAIL, P))
            z_high(0)
            act.wait_ge(comp_full, 3)
            act.activation(wvo_hi[:, :, :].rearrange("p k d -> p (k d)"), d_bank[0][:, :], ACT.Copy).then_inc(comp_hi, 1)
            squares(0, 0)
            squares(0, 1)
            act.wait_ge(w2_loaded, 32)
            abs_sums(PS, HC, slice(0, TAIL))
            u_high(0)
            act.wait_ge(w3_loaded, 16)
            for k in range(KD):
                act.activation(above3[:, k, 0:H], w3_n[:, k, :], ACT.Abs, accum_out=abs_part[:, 2 * PS + k:2 * PS + k + 1])\
                   .then_inc(part_ready, 1)
            x_high(1)
            z_high(1)
            u_high(1)
            drain_ternary(range(4))
            x2_high(0)
            drain_ternary(range(4, 9))

            def step(a, f, ahead, begun=False):
                if not begun:
                    z_high(a)
                gates(f, 0)
                if not begun:
                    u_high(a, (0,))
                hid_high(f, 0)
                if not begun:
                    u_high(a, (1,))
                for n in (1, 2):
                    gates(f, n)
                    hid_high(f, n)
                squares(a, 0)
                squares(a, 1)
                for n in (3, 4):
                    gates(f, n)
                    hid_high(f, n)
                gates(f, 5)
                if ahead:
                    x_high(a + 1)
                hid_high(f, 5)
                tail_stack(f)
                x2_high(a)

            step(1, 0, True, begun=True)
            with act.Fori(2, B - 1) as i:
                step(i, i - 1, True)
            step(B - 1, B - 2, False)
            last = B - 1
            for n in range(NU - 1):
                gates(last, n)
                if n < NU - 2:
                    hid_high(last, n)
            gates(last, NU - 1)
            hid_high(last, NU - 2)
            hid_high(last, NU - 1)
            tail_stack(last)

        @block.vector
        def _(dve):
            def block_stats(b, stats, stats_done, blocks=range(NB)):
                for j in blocks:
                    dve.bn_stats(stats[:, j, :], xblk(b, j)).then_inc(stats_done, 1)

            def moments(b, stats, stats_done, mv, mv_ready, blocks=range(NB)):
                wait_alone(dve, stats_done, b * NB + blocks[-1] + 1)
                for j in blocks:
                    dve.bn_aggr(mv[:, j, :], stats[:, j, :]).then_inc(mv_ready, 1)

            def normalise(b, mv, rstd, rstd_ready, xn, xn_ready, blocks=range(NB)):
                pieces = NB // len(blocks)
                dve.wait_ge(rstd_ready, b * pieces + blocks[0] * pieces // NB + 1)
                for j in blocks:
                    dve.tensor_scalar(xn[:, j, :], xblk(b, j), mv[:, j, 0:1], rstd[:, j:j + 1],
                                      ALU.subtract, ALU.mult).then_inc(xn_ready, 1)

            def low(b, stage, h, hi, dst):
                dve.wait_ge(a_hi, highs_of(b, stage, B - 1) + h + 1)
                dve.tensor_tensor(dst, a_bank[h][:, :], hi.bitcast(F32), ALU.subtract).then_inc(a_drained, 1)

            def x_low(b):
                for k in range(KD):
                    low(b, XT, k, xT_hi[:, k, :], xT_lo[:, k, :])

            def z_low(b):
                for m in range(KD):
                    low(b, ZT, m, z_hi[:, m, :], z_lo[:, m, :])

            def u_low(b):
                for h in range(2):
                    hs = slice(2 * h, 2 * h + 2)
                    low(b, UV, h, u_hi[:, hs, :].rearrange("p j d -> p (j d)"),
                        u_lo[:, hs, :].rearrange("p j d -> p (j d)"))

            def x2_low(b):
                for k in range(KD):
                    low(b, X2T, k, x2T_hi[:, k, :], x2T_lo[:, k, :])

            def mask(b, h):
                dve.wait_ge(a_full, turn_of(b, SC, B - 1) + h + 1)
                if not (isinstance(b, int) and b == 0):
                    dve.wait_ge(at_hi_ready, b * 2 + h - 1)
                cap = cap01[:, :, :, :].rearrange("p a c q -> p (a c q)") if h == 0 else \
                    cap23[:, :, :].rearrange("p a q -> p (a q)")
                cols = slice(0, 512) if h == 0 else slice(P, 512)
                dve.scalar_tensor_tensor(out=sc_pos[:, h, cols], in0=a_bank[h][:, cols], scalar=0.0, in1=cap,
                                         op0=ALU.max, op1=ALU.min).then_inc(a_drained, 1)

            def add_attention(b):
                for h in range(2):
                    dve.wait_ge(a_full, turn_of(b, YA, B - 1) + h + 1)
                    dve.tensor_tensor(xblk(b, 2 * h, 2), a_bank[h][:, :], xblk(b, 2 * h, 2), ALU.add).then_inc(a_drained, 1)
                    if h == 1:
                        moments(b, stats2, stats2_done, mv2, mv2_ready, (0, 1))
                    wait_alone(dve, a_drained, turn_of(b, YA, B - 1) + h + 1)
                    block_stats(b, stats2, stats2_done, (2 * h, 2 * h + 1))
                moments(b, stats2, stats2_done, mv2, mv2_ready, (2, 3))

            def hidden(b, n):
                dve.wait_ge(gate_ready, b * NU + n + 1)
                if not (isinstance(b, int) and b == 0 and n < 2):
                    dve.wait_ge(hid_lo_ready, b * NU + n - 1)
                if n == HC % 2 and not (isinstance(b, int) and b == 0):
                    dve.wait_ge(hid_hi_ready, b * (NU + 1))
                rows = slice(0, P) if n < HC else slice(0, TAIL)
                dve.tensor_tensor(hid[rows, n % 2, :], up_bank[n % 2][1 if n < HC else 0][rows, :], gate[rows, n % 2, :],
                                  ALU.mult).then_inc(hid_ready, 1)

            def add_ffn(b):
                for h in range(2):
                    dve.wait_ge(d_full, b * 2 + h + 1)
                    dve.tensor_tensor(xblk(b, 2 * h, 2), d_bank[h][:, :], xblk(b, 2 * h, 2), ALU.add).then_inc(out_ready, 1)

            dve.memset(abs_part[:, :], 0.0).then_inc(part_zeroed, 1)
            dve.wait_ge(x_loaded, 16)
            block_stats(0, stats1, stats1_done)
            moments(0, stats1, stats1_done, mv1, mv1_ready)
            normalise(0, mv1, rstd1, rstd1_ready, xn1, xn1_ready)
            dve.wait_ge(comp_hi, 1)
            dve.tensor_tensor(m_lo[:, :, :].rearrange("p k d -> p (k d)"), d_bank[0][:, :],
                              m_hi[:, :, :].rearrange("p k d -> p (k d)").bitcast(F32), ALU.subtract).then_inc(comp_done, 1)
            x_low(0)
            dve.wait_ge(x_loaded, 32)
            block_stats(1, stats1, stats1_done)
            moments(1, stats1, stats1_done, mv1, mv1_ready)
            z_low(0)
            normalise(1, mv1, rstd1, rstd1_ready, xn1, xn1_ready)
            dve.wait_ge(comp_hi, 2)
            dve.tensor_tensor(wvo_lo[:, :, :].rearrange("p k d -> p (k d)"), d_bank[0][:, :],
                              wvo_hi[:, :, :].rearrange("p k d -> p (k d)").bitcast(F32), ALU.subtract).then_inc(comp_done, 1)
            dve.wait_ge(caps_ready, 4)
            mask(0, 0)
            mask(0, 1)
            u_low(0)
            dve.wait_ge(comp_full, 4)
            dve.tensor_reduce(abs_total[:, :], d_bank[1][:, 0:3 * PS].rearrange("p (w c) -> p w c", w=3), AX_X,
                              ALU.add).then_inc(total_ready, 1)
            dve.wait_ge(total_ready, 1)
            half_mean, half_eps = 0.5 / (H * D), 0.5 * QUANT_EPS
            for t, sign in ((thr, 1.0), (nthr, -1.0)):
                dve.tensor_scalar(t[:, 0:3], abs_total[:, :], sign * half_mean, sign * half_eps, ALU.mult, ALU.add)\
                   .then_inc(thr_ready, 1)
                for rows, c in ((slice(TAIL, P), 0), (slice(0, TAIL), 1)):
                    dve.tensor_scalar(t[rows, 3:4], abs_total[rows, c:c + 1], sign * half_mean, sign * half_eps,
                                      ALU.mult, ALU.add).then_inc(thr_ready, 1)
            dve.wait_ge(thr_ready, 6)

            def ternary(above, below, src, c):
                dve.tensor_scalar(above, src, thr[:, c:c + 1], None, ALU.is_gt).then_inc(ternary_ready, 1)
                if below is not None:
                    dve.tensor_scalar(below, src, nthr[:, c:c + 1], None, ALU.is_lt).then_inc(ternary_ready, 1)

            ternary(above12[:, 0:HC, :], below12[:, 0:HC, :], w12_n[:, 0:HC, :], 0)
            x_low(1)
            add_attention(0)
            ternary(above12[:, HC:2 * HC, :], below12[:, HC:2 * HC, :], w12_n[:, HC:2 * HC, :], 1)
            z_low(1)
            normalise(0, mv2, rstd2, rstd2_ready, xn2, xn2_ready, (0, 1))
            normalise(0, mv2, rstd2, rstd2_ready, xn2, xn2_ready, (2, 3))
            ternary(above12[:, 2 * HC, :], below12[:, 2 * HC, :], w12_n[:, 2 * HC, :], 3)
            u_low(1)
            x2_low(0)
            ternary(above3[:, :, 0:H], None, w3_n[:, :, :], 2)
            ternary(above3[:, :, H:H3], None, w3_n[:, :, HC * P:H], 2)

            def step(a, f, ahead, begun=False):
                if not begun:
                    z_low(a)
                hidden(f, 0)
                if ahead:
                    wait_alone(dve, x_loaded, 16 * a + 32)
                    block_stats(a + 1, stats1, stats1_done)
                    moments(a + 1, stats1, stats1_done, mv1, mv1_ready)
                if not begun:
                    u_low(a)
                hidden(f, 1)
                if ahead:
                    normalise(a + 1, mv1, rstd1, rstd1_ready, xn1, xn1_ready)
                hidden(f, 2)
                mask(a, 0)
                mask(a, 1)
                hidden(f, 3)
                hidden(f, 4)
                add_attention(a)
                normalise(a, mv2, rstd2, rstd2_ready, xn2, xn2_ready, (0, 1))
                hidden(f, 5)
                normalise(a, mv2, rstd2, rstd2_ready, xn2, xn2_ready, (2, 3))
                if ahead:
                    x_low(a + 1)
                x2_low(a)
                add_ffn(f)

            step(1, 0, True, begun=True)
            with dve.Fori(2, B - 1) as i:
                step(i, i - 1, True)
            step(B - 1, B - 2, False)
            last = B - 1
            for n in range(NU):
                hidden(last, n)
            for n in (NU - 2, NU - 1):
                dve.wait_ge(hid_hi_ready, last * (NU + 1) + n + 1)
                o, i, h = low_of(n)
                dve.tensor_tensor(o, i, h.bitcast(F32), ALU.subtract).then_inc(hid_lo_last, 1)
            add_ffn(last)

        @block.gpsimd
        def _(pool):
            def inv_std(n, mv, mv_ready, veps, veps_ready, rstd, rstd_ready, pieces, piece):
                js = slice(piece * NB // pieces, (piece + 1) * NB // pieces)
                wait_alone(pool, mv_ready, n * (NB // pieces) + NB // pieces)
                pool.tensor_scalar(veps[:, js], mv[:, js, 1], LN_EPS, None, ALU.add).then_inc(veps_ready, 1)
                pool.wait_ge(veps_ready, n + 1)
                pool.tensor_tensor(rstd[:, js], veps[:, js], neg_half[:, js], ALU.pow).then_inc(rstd_ready, 1)

            def inv_std1(b):
                inv_std(b, mv1, mv1_ready, veps1, veps1_ready, rstd1, rstd1_ready, 1, 0)

            def inv_std2(b):
                for piece in range(2):
                    inv_std(b * 2 + piece, mv2, mv2_ready, veps2, veps2_ready, rstd2, rstd2_ready, 2, piece)

            def hid_low(b, n):
                pool.wait_ge(hid_hi_ready, b * (NU + 1) + n + 1)
                o, i, h = low_of(n)
                pool.tensor_tensor(o, i, h.bitcast(F32), ALU.subtract).then_inc(hid_lo_ready, 1)

            def at_low(b):
                for h in range(2):
                    cols = slice(0, 512) if h == 0 else slice(P, 512)
                    pool.wait_ge(sq_ready, b * 2 + h + 1)
                    pool.wait_ge(at_hi_ready, b * 2 + h + 1)
                    pool.tensor_tensor(at_lo[:, h, cols], sc_sq[:, h, cols], at_hi[:, h, cols].bitcast(F32),
                                       ALU.subtract).then_inc(at_lo_ready, 1)

            pool.memset(ident[:, :], 0.0).then_inc(zeroed, 1)
            pool.memset(neg_half[:, :], -0.5).then_inc(zeroed, 1)
            pool.memset(ones[:, :], 1.0).then_inc(zeroed, 1)
            pool.wait_ge(zeroed, 3)
            pool.affine_select(out=ident[:, :], in_=ident[:, :], compare_op=ALU.not_equal, fill=1.0, base=0,
                               pattern=[[-1, P]], channel_multiplier=1).then_inc(consts_ready, 1)
            inv_std1(0)
            pool.memset(cap01[:, :, :, :], BIG).then_inc(zeroed, 1)
            pool.memset(cap23[:, :, :], BIG).then_inc(zeroed, 1)
            pool.wait_ge(zeroed, 5)
            same = dict(compare_op=ALU.is_ge, fill=0.0, base=0, channel_multiplier=-1)
            before = dict(compare_op=ALU.is_ge, fill=0.0, base=0, channel_multiplier=1)
            pool.affine_select(out=cap01[:, :, 0, :], in_=cap01[:, :, 0, :], pattern=[[0, 2], [1, P]], **same).then_inc(caps_ready, 1)
            pool.affine_select(out=cap01[:, :, 1, :], in_=cap01[:, :, 1, :], pattern=[[0, 2], [-1, P]], **before).then_inc(caps_ready, 1)
            pool.affine_select(out=cap23[:, 0:2, :], in_=cap23[:, 0:2, :], pattern=[[0, 2], [1, P]], **same).then_inc(caps_ready, 1)
            pool.affine_select(out=cap23[:, 2, :], in_=cap23[:, 2, :], pattern=[[-1, P]], **before).then_inc(caps_ready, 1)
            pool.wait_ge(consts_ready, 1)
            pool.tensor_copy(ident_bf[:, :], ident[:, :]).then_inc(consts_ready, 1)
            pool.tensor_scalar(nident_bf[:, :], ident[:, :], -1.0, None, ALU.mult).then_inc(consts_ready, 1)
            inv_std1(1)
            at_low(0)
            pool.wait_ge(w3_loaded, 16)
            pool.wait_ge(thr_ready, 6)
            pool.tensor_scalar(below3[:, :, H:H3], w3_n[:, :, HC * P:H], nthr[:, 2:3], None, ALU.is_lt)\
                .then_inc(below3_ready, 1)
            inv_std2(0)
            pool.tensor_scalar(below3[:, :, 0:H], w3_n[:, :, :], nthr[:, 2:3], None, ALU.is_lt).then_inc(below3_ready, 1)

            def step(a, f, ahead):
                hid_low(f, 0)
                if ahead:
                    inv_std1(a + 1)
                hid_low(f, 1)
                hid_low(f, 2)
                at_low(a)
                hid_low(f, 3)
                hid_low(f, 4)
                inv_std2(a)
                hid_low(f, 5)

            step(1, 0, True)
            with pool.Fori(2, B - 1) as i:
                step(i, i - 1, True)
            step(B - 1, B - 2, False)
            for n in range(NU - 2):
                hid_low(B - 1, n)


_INS = ['L0_attn_x', 'L0_attn_w_attn', 'L0_attn_w_o', 'L0_ffn_w1', 'L0_ffn_w2', 'L0_ffn_w3']


def kernel(**inputs):
    import numpy as _np
    import concourse.bacc as _bacc
    from concourse import mybir as _mybir
    from concourse.bass_utils import run_bass_kernel_spmd as _run

    nc = _bacc.Bacc("TRN2", target_bir_lowering=False, num_devices=1)
    arrays, args = {}, []
    for name in _INS:
        a = _np.ascontiguousarray(inputs[name])
        arrays[f"in_{name}_dram"] = a
        args.append(nc.dram_tensor(f"in_{name}_dram", a.shape, _mybir.dt.from_np(a.dtype), kind="ExternalInput").ap())
    shape = inputs['L0_attn_x'].shape
    args.append(nc.dram_tensor("out_0_dram", shape, _mybir.dt.float32, kind="ExternalOutput").ap())
    build(nc, *args)
    r = _run(nc, [arrays], core_ids=[0])
    return r.results[0]["out_0_dram"]
```

```python
from contextlib import ExitStack

import concourse.bass as bass
from concourse import mybir

P = 128
F32 = mybir.dt.float32
F32R = mybir.dt.float32r
BF16 = mybir.dt.bfloat16
ALU = mybir.AluOpType
ACT = mybir.ActivationFunctionType
AX_X = mybir.AxisListType.X

LN_EPS = 1e-5
QUANT_EPS = 1e-8
BIG = 3.4028234663852886e38

ZT, UV, SC, YA, XT, X2T = range(6)
A_USES = 12
FIRST_TURNS = {(0, XT): 0, (0, ZT): 2, (0, UV): 4, (1, XT): 6, (0, SC): 8, (1, ZT): 10, (0, YA): 12, (1, UV): 14,
               (0, X2T): 16}
FIRST_HIGHS = {(0, XT): 0, (0, ZT): 2, (0, UV): 4, (1, XT): 6, (1, ZT): 8, (1, UV): 10, (0, X2T): 12}


def turn_of(b, stage, last):
    if isinstance(b, int) and (b, stage) in FIRST_TURNS:
        return FIRST_TURNS[b, stage]
    if stage == XT:
        return b * A_USES - 2
    if stage == X2T:
        return b * A_USES + (10 if isinstance(b, int) and b == last else 12)
    return b * A_USES + 2 + 2 * stage


def highs_of(b, stage, last):
    if isinstance(b, int) and (b, stage) in FIRST_HIGHS:
        return FIRST_HIGHS[b, stage]
    if stage == XT:
        return b * 8 - 2
    if stage == X2T:
        return b * 8 + (6 if isinstance(b, int) and b == last else 8)
    return b * 8 + 2 + 2 * stage


def build(nc, x, w_attn, w_o, w1, w2, w3, out):
    B, T, D = x.shape
    H = w1.shape[0]
    NB = T // P
    KD = D // P
    HC = H // P
    TAIL = H - HC * P
    assert NB == 4 and KD == 2 and TAIL == 64 and T == 512
    XB = NB * D
    NCH = 2 * HC + 1
    NU = HC + 1
    PS = 2
    WINDOW = float(P)

    x_dram = x.rearrange("b (j p) d -> p b j d", p=P)
    out_dram = out.rearrange("b (j p) d -> p b j d", p=P)

    with ExitStack() as ctx:
        def sb(name, shape, dt=F32):
            return ctx.enter_context(nc.sbuf_tensor(name, shape, dt))

        def bank(name):
            return ctx.enter_context(nc.psum_tensor(name, [P, 512], F32))

        def sem(name):
            return ctx.enter_context(nc.semaphore(name))

        xs = sb("xs", [P, B * XB])
        wat = sb("wat", [P, 3 * KD, D])
        wo_n = sb("wo_n", [P, KD, D])
        woT = sb("woT", [P, KD, D])
        w12_n = sb("w12_n", [P, NCH, D])
        w3_n = sb("w3_n", [P, KD, H])
        m_hi, m_lo = sb("m_hi", [P, KD, D], F32R), sb("m_lo", [P, KD, D], F32R)
        wvo_hi, wvo_lo = sb("wvo_hi", [P, KD, D], F32R), sb("wvo_lo", [P, KD, D], F32R)
        above12, below12 = sb("above12", [P, NCH, D], BF16), sb("below12", [P, NCH, D], BF16)
        H3 = (HC + 1) * P
        above3, below3 = sb("above3", [P, KD, H3], BF16), sb("below3", [P, KD, H3], BF16)
        w12T = sb("w12T", [P, KD, NCH, P], F32R)
        w3T = sb("w3T", [P, HC + 1, D], F32R)
        abs_part = sb("abs_part", [P, 3 * PS])
        abs_total = sb("abs_total", [P, 3])
        thr, nthr = sb("thr", [P, 4]), sb("nthr", [P, 4])
        ident = sb("ident", [P, P])
        ident_bf, nident_bf = sb("ident_bf", [P, P], BF16), sb("nident_bf", [P, P], BF16)
        ones = sb("ones", [P, P])
        neg_half = sb("neg_half", [P, NB])
        cap01 = sb("cap01", [P, 2, 2, P])
        cap23 = sb("cap23", [P, 3, P])

        stats1, stats2 = sb("stats1", [P, NB, 6]), sb("stats2", [P, NB, 6])
        mv1, mv2 = sb("mv1", [P, NB, 2]), sb("mv2", [P, NB, 2])
        veps1, veps2 = sb("veps1", [P, NB]), sb("veps2", [P, NB])
        rstd1, rstd2 = sb("rstd1", [P, NB]), sb("rstd2", [P, NB])
        xn1, xn2 = sb("xn1", [P, NB, D]), sb("xn2", [P, NB, D])
        xT_hi, xT_lo = sb("xT_hi", [P, KD, T], F32R), sb("xT_lo", [P, KD, T], F32R)
        x2T_hi, x2T_lo = sb("x2T_hi", [P, KD, T], F32R), sb("x2T_lo", [P, KD, T], F32R)
        z_hi, z_lo = sb("z_hi", [P, KD, T], F32R), sb("z_lo", [P, KD, T], F32R)
        u_hi, u_lo = sb("u_hi", [P, NB, D], F32R), sb("u_lo", [P, NB, D], F32R)
        sc_pos = sb("sc_pos", [P, 2, 512])
        sc_sq = sb("sc_sq", [P, 2, 512])
        at_hi, at_lo = sb("at_hi", [P, 2, 512], F32R), sb("at_lo", [P, 2, 512], F32R)
        gate = sb("gate", [P, 2, T])
        hid = sb("hid", [P, 2, T])
        hid_hi, hid_lo = sb("hid_hi", [P, HC, T], F32R), sb("hid_lo", [P, HC, T], F32R)
        tail_hi = sb("tail_hi", [TAIL, T], F32R)
        tail_st = sb("tail_st", [P, T], F32R)

        a_bank = [bank("a_bank0"), bank("a_bank1")]
        up_bank = [[bank(f"up{r}_{g}") for g in range(2)] for r in range(2)]
        d_bank = [bank("d_bank0"), bank("d_bank1")]

        x0_half_loaded, x_loaded = sem("x0_half_loaded"), sem("x_loaded")
        wat_loaded, wo_loaded, wv_loaded = sem("wat_loaded"), sem("wo_loaded"), sem("wv_loaded")
        w1_loaded, w2_loaded, w3_loaded = sem("w1_loaded"), sem("w2_loaded"), sem("w3_loaded")
        zeroed, consts_ready, caps_ready = sem("zeroed"), sem("consts_ready"), sem("caps_ready")
        comp_full = sem("comp_full")
        comp_hi, comp_done = sem("comp_hi"), sem("comp_done")
        wo_turned = sem("wo_turned")
        part_zeroed, part_ready = sem("part_zeroed"), sem("part_ready")
        total_ready, thr_ready = sem("total_ready"), sem("thr_ready")
        ternary_ready, below3_ready = sem("ternary_ready"), sem("below3_ready")
        tails_ready = sem("tails_ready")
        prep_full, prep_drained = sem("prep_full"), sem("prep_drained")
        stats1_done, mv1_ready, veps1_ready, rstd1_ready, xn1_ready = (
            sem("stats1_done"), sem("mv1_ready"), sem("veps1_ready"), sem("rstd1_ready"), sem("xn1_ready"))
        stats2_done, mv2_ready, veps2_ready, rstd2_ready, xn2_ready = (
            sem("stats2_done"), sem("mv2_ready"), sem("veps2_ready"), sem("rstd2_ready"), sem("xn2_ready"))
        a_full = sem("a_full")
        a_hi = sem("a_hi")
        a_drained = sem("a_drained")
        sq_ready, at_hi_ready, at_lo_ready = sem("sq_ready"), sem("at_hi_ready"), sem("at_lo_ready")
        up_full, gate_ready = sem("up_full"), sem("gate_ready")
        hid_ready = sem("hid_ready")
        hid_hi_ready, hid_lo_ready, hid_lo_last = sem("hid_hi_ready"), sem("hid_lo_ready"), sem("hid_lo_last")
        d_full, out_ready = sem("d_full"), sem("out_ready")
        stored = sem("stored")
        waits_alone = sem("waits_alone")

        block = ctx.enter_context(nc.Block())

        def wait_alone(eng, what, count):
            eng.wait_ge(what, count)
            eng.sem_inc(waits_alone, 1)

        nb12 = KD * NCH
        FILLS12 = [(0, 4), (NCH + 1, NCH + HC)] + [(4, 8), (8, 12)] + [(NCH + HC, NCH + HC + 4), (NCH + HC + 4, nb12)]
        N_FILLS = len(FILLS12) + KD * (HC + 1) // 4
        FILL_BANKS = [up_bank[0][0], up_bank[0][1], up_bank[1][0], up_bank[1][1], up_bank[0][0], up_bank[1][0],
                      d_bank[0], d_bank[1], d_bank[0]]

        def fill_range(n):
            lo = 4 * (n - len(FILLS12))
            return FILLS12[n] if n < len(FILLS12) else (lo, lo + 4)

        def ternary_blocks(n):
            lo, hi = fill_range(n)
            if n < len(FILLS12):
                return [(above12[:, c, k * P:(k + 1) * P], below12[:, c, k * P:(k + 1) * P])
                        for k, c in (divmod(i, NCH) for i in range(lo, hi))]
            return [(above3[:, k, c * P:(c + 1) * P], below3[:, k, c * P:(c + 1) * P])
                    for c, k in (divmod(i, KD) for i in range(lo, hi))]

        def bank_of(b, stage, h):
            if isinstance(b, int) and (b, stage) == (1, XT):
                return up_bank[1][h]
            if isinstance(b, int) and (b, stage) == (0, X2T):
                return d_bank[h]
            return a_bank[h]

        def xT_of(b):
            return (x2T_hi, x2T_lo) if isinstance(b, int) and b == 0 else (xT_hi, xT_lo)

        def low_of(n):
            if n < HC:
                return hid_lo[:, n, :], hid[:, n % 2, :], hid_hi[:, n, :]
            return tail_st[0:TAIL, :], hid[0:TAIL, n % 2, :], tail_hi[0:TAIL, :]

        def xblk(b, j, n=1):
            return xs[:, bass.ds(b * XB + j * D, n * D)]

        @block.sync
        def _(sp):
            sp.dma_start(xblk(0, 0, 2).rearrange("p (j d) -> p j d", j=2), x_dram[:, 0, 0:2]).then_inc(x0_half_loaded, 16)
            sp.dma_start(wat[:, 0:2 * KD, :], w_attn[0:2 * D, :].rearrange("(c p) d -> p c d", p=P)).then_inc(wat_loaded, 16)
            sp.wait_ge(x_loaded, 16)
            sp.dma_start(w12_n[:, 0:HC, :], w1[0:HC * P, :].rearrange("(c p) d -> p c d", p=P)).then_inc(w1_loaded, 16)
            sp.dma_start(w12_n[TAIL:P, 2 * HC, :], w1[HC * P:H, :]).then_inc(w1_loaded, 16)
            sp.dma_start(xblk(1, 0, NB).rearrange("p (j d) -> p j d", j=NB), x_dram[:, 1]).then_inc(x_loaded, 16)
            sp.dma_start(w12_n[:, HC:2 * HC, :], w2[0:HC * P, :].rearrange("(c p) d -> p c d", p=P)).then_inc(w2_loaded, 16)
            sp.dma_start(w12_n[0:TAIL, 2 * HC, :], w2[HC * P:H, :]).then_inc(w2_loaded, 16)
            sp.dma_start(w3_n[:, :, :], w3.rearrange("(c p) h -> p c h", p=P)).then_inc(w3_loaded, 16)
            with sp.Fori(2, B) as i:
                sp.wait_ge(x_loaded, 16 * i)
                dst = xs[:, bass.ds(i * XB, XB)].rearrange("p (j d) -> p j d", j=NB)
                src = x_dram[:, bass.ds(i, 1)].rearrange("p o j d -> p (o j) d")
                sp.dma_start(dst, src).then_inc(x_loaded, 16)
            with sp.Fori(0, B - 1) as i:
                sp.wait_ge(out_ready, 2 * i + 2)
                dst = out_dram[:, bass.ds(i, 1)].rearrange("p o j d -> p (o j) d")
                src = xs[:, bass.ds(i * XB, XB)].rearrange("p (j d) -> p j d", j=NB)
                sp.dma_start(dst, src).then_inc(stored, 16)
            for h in range(2):
                sp.wait_ge(out_ready, 2 * B - 1 + h)
                sp.dma_start(out_dram[:, B - 1, 2 * h:2 * h + 2], xblk(B - 1, 2 * h, 2).rearrange("p (j d) -> p j d", j=2))\
                  .then_inc(stored, 16)
            sp.wait_ge(stored, 16 * (B + 1))

        @block.tensor
        def _(pe):
            def a_take(b, stage, h, need=None):
                if isinstance(b, int) and (b, stage) in ((1, XT), (0, X2T)):
                    return bank_of(b, stage, h)
                if isinstance(b, int) and (b, stage) == (0, SC):
                    pe.wait_ge(a_drained, turn_of(b, UV, B - 1) + h + 1)
                    return a_bank[h]
                drained = turn_of(b, stage, B - 1) + h - 1
                if need is not None:
                    b0 = b if isinstance(b, int) else 3
                    if turn_of(b0, need, B - 1) + 2 > turn_of(b0, stage, B - 1) + h - 1:
                        drained = turn_of(b, need, B - 1) + 2
                if not (isinstance(drained, int) and drained <= 0):
                    pe.wait_ge(a_drained, drained)
                return a_bank[h]

            def turn(b, stage, xn, xn_ready, chunks=range(KD)):
                for k in chunks:
                    bk = a_take(b, stage, k)
                    for j in range(NB):
                        if k == 0:
                            pe.wait_ge(xn_ready, b * NB + j + 1)
                        last = pe.transpose(bk[:, j * P:(j + 1) * P], xn[:, j, k * P:(k + 1) * P], ident[:, :])
                    last.then_inc(a_full, 1)

            def three(out_ap, terms):
                n = len(terms) * 3
                at = 0
                for lh, ll, rh, rl in terms:
                    for l, r in ((lh, rh), (lh, rl), (ll, rh)):
                        last = pe.matmul(out_ap, l, r, start=(at == 0), stop=(at == n - 1))
                        at += 1
                return last

            def z_products(b):
                x_hi, x_lo = xT_of(b)
                for m in range(KD):
                    bk = a_take(b, ZT, m, need=XT)
                    ms = slice(m * P, (m + 1) * P)
                    three(bk[:, :], [(m_hi[:, k, ms], m_lo[:, k, ms], x_hi[:, k, :], x_lo[:, k, :])
                                     for k in range(KD)]).then_inc(a_full, 1)

            def u_products(b):
                x_hi, x_lo = xT_of(b)
                for h in range(2):
                    bk = a_take(b, UV, h)
                    for j in (2 * h, 2 * h + 1):
                        js = slice(j * P, (j + 1) * P)
                        last = three(bk[:, (j % 2) * D:(j % 2 + 1) * D],
                                     [(x_hi[:, k, js], x_lo[:, k, js], wvo_hi[:, k, :], wvo_lo[:, k, :])
                                      for k in range(KD)])
                    last.then_inc(a_full, 1)

            def scores(b):
                x_hi, x_lo = xT_of(b)
                for h, parts in enumerate(([(0, 0, 0), (1, P, 2 * P)], [(3, 2 * P, 0), (2, 2 * P, 2 * P)])):
                    bk = a_take(b, SC, h, need=ZT)
                    for j, q0, c0 in parts:
                        js, qs = slice(j * P, (j + 1) * P), slice(q0, q0 + 2 * P)
                        last = three(bk[:, c0:c0 + 2 * P],
                                     [(x_hi[:, k, js], x_lo[:, k, js], z_hi[:, k, qs], z_lo[:, k, qs])
                                      for k in range(KD)])
                    last.then_inc(a_full, 1)

            AT = {(0, 0): (0, 0), (0, 1): (0, P), (1, 1): (0, 2 * P), (1, 2): (0, 3 * P),
                  (3, 3): (1, P), (2, 2): (1, 2 * P), (2, 3): (1, 3 * P)}

            def attend(b):
                for h in range(2):
                    bk = a_take(b, YA, h, need=UV)
                    pe.wait_ge(at_lo_ready, b * 2 + h + 1)
                    for i in (2 * h, 2 * h + 1):
                        terms = []
                        for j in ([i - 1] if i else []) + [i]:
                            g, c = AT[(j, i)]
                            terms.append((at_hi[:, g, c:c + P], at_lo[:, g, c:c + P], u_hi[:, j, :], u_lo[:, j, :]))
                        last = three(bk[:, (i % 2) * D:(i % 2 + 1) * D], terms)
                    last.then_inc(a_full, 1)

            def up(b, n):
                if isinstance(b, int) and b == 0 and n in (0, 1):
                    pe.wait_ge(prep_drained, len(FILLS12) - (n == 0))
                if n == 0:
                    pe.wait_ge(a_drained, turn_of(b, X2T, B - 1) + 2)
                if not (isinstance(b, int) and b == 0 and n < 2):
                    pe.wait_ge(hid_ready, b * NU + n - 1)
                chunks = [n, HC + n] if n < HC else [2 * HC]
                for g, c in enumerate(chunks):
                    at = 0
                    for k in range(KD):
                        for part in (x2T_hi, x2T_lo):
                            last = pe.matmul(up_bank[n % 2][g][:, :], w12T[:, k, c, :], part[:, k, :],
                                             start=(at == 0), stop=(at == 2 * KD - 1))
                            at += 1
                last.then_inc(up_full, 1)

            def down(b, n, tokens=range(NB)):
                if isinstance(b, int) and b == B - 1 and n >= NU - 2:
                    pe.wait_ge(hid_lo_last, n - (NU - 2) + 1)
                else:
                    pe.wait_ge(hid_lo_ready, b * NU + n + 1)
                if n == HC:
                    pe.wait_ge(hid_hi_ready, b * (NU + 1) + NU + 1)
                for j in tokens:
                    if n == 0 and j % 2 == 0 and not (isinstance(b, int) and b == 0):
                        pe.wait_ge(out_ready, b * 2 + j // 2 - 1)
                    js = slice(j * P, (j + 1) * P)
                    parts = [hid_hi[:, n, js], hid_lo[:, n, js]] if n < HC else [tail_st[:, js]]
                    for q, part in enumerate(parts):
                        last = pe.matmul(d_bank[j // 2][:, (j % 2) * D:(j % 2 + 1) * D], part, w3T[:, n, :],
                                         start=(n == 0 and j % 2 == 0 and q == 0), stop=(n == NU - 1 and q == len(parts) - 1),
                                         skip_group_check=True)
                    if n == NU - 1 and j % 2 == 1:
                        last.then_inc(d_full, 1)

            def turn_ternary(ns):
                for n in ns:
                    before = [m for m in range(n) if FILL_BANKS[m] is FILL_BANKS[n]]
                    if before:
                        pe.wait_ge(prep_drained, before[-1] + 1)
                    for q, (hi, lo) in enumerate(ternary_blocks(n)):
                        o = FILL_BANKS[n][:, q * P:(q + 1) * P]
                        pe.matmul(o, hi, ident_bf[:, :], start=True, stop=False)
                        last = pe.matmul(o, lo, nident_bf[:, :], start=False, stop=True)
                    last.then_inc(prep_full, 1)

            def compose(bk, lhs, rhs):
                for k in range(KD):
                    for c in range(KD):
                        last = pe.matmul(bk[:, k * D:(k + 1) * D], lhs(c)[:, k * P:(k + 1) * P], rhs(c),
                                         start=(c == 0), stop=(c == KD - 1))
                last.then_inc(comp_full, 1)

            def abs_sum(w):
                c0, c1 = w * PS, (w + 1) * PS
                pe.wait_ge(part_ready, c1)
                pe.matmul(d_bank[1][:, c0:c1], ones[:, :], abs_part[:, c0:c1], start=True, stop=True).then_inc(comp_full, 1)

            pe.wait_ge(zeroed, 3)
            for _ in range(10):
                pe.matmul(up_bank[0][0][:, 0:P], ones[:, :], ones[:, :], start=True, stop=True)
            pe.wait_ge(wat_loaded, 16)
            compose(d_bank[0], lambda c: wat[:, c, :], lambda c: wat[:, KD + c, :])
            pe.wait_ge(consts_ready, 1)
            pe.wait_ge(wo_loaded, 16)
            for e in range(KD):
                for c in range(KD):
                    last = pe.transpose(d_bank[1][:, e * D + c * P:e * D + (c + 1) * P], wo_n[:, c, e * P:(e + 1) * P],
                                        ident[:, :])
            last.then_inc(comp_full, 1)
            turn(0, XT, xn1, xn1_ready)
            pe.wait_ge(wo_turned, 1)
            pe.wait_ge(wv_loaded, 16)
            pe.wait_ge(comp_done, 1)
            compose(d_bank[0], lambda c: wat[:, 2 * KD + c, :], lambda c: woT[:, c, :])
            z_products(0)
            abs_sum(0)
            pe.wait_ge(comp_done, 2)
            u_products(0)
            turn(1, XT, xn1, xn1_ready)
            abs_sum(1)
            scores(0)
            z_products(1)
            pe.wait_ge(consts_ready, 3)
            pe.wait_ge(ternary_ready, 2)
            turn_ternary((0, 1))
            attend(0)
            abs_sum(2)
            u_products(1)
            pe.wait_ge(ternary_ready, 4)
            turn_ternary((2,))
            pe.wait_ge(total_ready, 3)
            turn(0, X2T, xn2, xn2_ready)
            pe.wait_ge(tails_ready, 2)
            turn_ternary(range(3, len(FILLS12)))

            def step(a, f, ahead, begun=False):
                if not begun:
                    z_products(a)
                up(f, 0)
                if not begun:
                    u_products(a)
                if begun:
                    pe.wait_ge(ternary_ready, 6)
                    pe.wait_ge(below3_ready, 2)
                    turn_ternary((len(FILLS12), len(FILLS12) + 1))
                up(f, 1)
                if begun:
                    turn_ternary((len(FILLS12) + 2,))
                up(f, 2)
                scores(a)
                up(f, 3)
                up(f, 4)
                attend(a)
                if begun:
                    pe.wait_ge(prep_drained, N_FILLS)
                down(f, 0)
                up(f, 5)
                if ahead:
                    turn(a + 1, XT, xn1, xn1_ready)
                down(f, 1)
                down(f, 2)
                down(f, 3)
                if ahead:
                    down(f, 4, (0,))
                    turn(a, X2T, xn2, xn2_ready, (0,))
                    down(f, 4, (1, 2))
                    turn(a, X2T, xn2, xn2_ready, (1,))
                    down(f, 4, (3,))
                else:
                    turn(a, X2T, xn2, xn2_ready)
                    down(f, 4)
                down(f, 5)

            step(1, 0, True, begun=True)
            with pe.Fori(2, B - 1) as i:
                step(i, i - 1, True)
            step(B - 1, B - 2, False)
            last = B - 1
            for n in range(NU):
                up(last, n)
            for n in (0, 1, 2):
                down(last, n)
            for tokens in ((0, 1), (2, 3)):
                for n in (3, 4, 5):
                    down(last, n, tokens)

        @block.scalar
        def _(act):
            def high_pair(b, stage, dst, halves=range(2)):
                for h in halves:
                    act.wait_ge(a_full, turn_of(b, stage, B - 1) + h + 1)
                    act.activation(dst(h), bank_of(b, stage, h)[:, :], ACT.Copy).then_inc(a_hi, 1)

            def x_high(b):
                high_pair(b, XT, lambda k: xT_of(b)[0][:, k, :])

            def z_high(b):
                high_pair(b, ZT, lambda m: z_hi[:, m, :])

            def u_high(b, halves=range(2)):
                high_pair(b, UV, lambda h: u_hi[:, 2 * h:2 * h + 2, :].rearrange("p j d -> p (j d)"), halves)

            def x2_high(b):
                high_pair(b, X2T, lambda k: x2T_hi[:, k, :])

            def squares(b, h):
                cols = slice(0, 512) if h == 0 else slice(P, 512)
                act.wait_ge(a_drained, turn_of(b, SC, B - 1) + h + 1)
                if not (isinstance(b, int) and b == 0):
                    act.wait_ge(at_lo_ready, b * 2 + h - 1)
                act.activation(sc_sq[:, h, cols], sc_pos[:, h, cols], ACT.Square, scale=1.0 / WINDOW).then_inc(sq_ready, 1)
                act.activation(at_hi[:, h, cols], sc_pos[:, h, cols], ACT.Square, scale=1.0 / WINDOW).then_inc(at_hi_ready, 1)

            def gates(b, n):
                act.wait_ge(up_full, b * NU + n + 1)
                if not (isinstance(b, int) and b == 0 and n < 2):
                    act.wait_ge(hid_ready, b * NU + n - 1)
                if n < HC:
                    g = act.activation(gate[:, n % 2, :], up_bank[n % 2][0][:, :], ACT.Sigmoid)
                else:
                    g = act.activation(gate[0:TAIL, n % 2, :], up_bank[n % 2][0][TAIL:P, :], ACT.Sigmoid)
                g.then_inc(gate_ready, 1)

            def hid_high(b, n):
                act.wait_ge(hid_ready, b * NU + n + 1)
                if n < HC:
                    act.activation(hid_hi[:, n, :], hid[:, n % 2, :], ACT.Copy).then_inc(hid_hi_ready, 1)
                else:
                    act.activation(tail_hi[0:TAIL, :], hid[0:TAIL, n % 2, :], ACT.Copy).then_inc(hid_hi_ready, 1)

            def tail_stack(b):
                act.activation(tail_st[TAIL:P, :], hid[0:TAIL, HC % 2, :], ACT.Copy).then_inc(hid_hi_ready, 1)

            def drain_ternary(ns):
                for n in ns:
                    act.wait_ge(prep_full, n + 1)
                    lo, hi = fill_range(n)
                    dst = w12T[:, :, :, :].rearrange("p k c q -> p (k c q)") if n < len(FILLS12) else \
                        w3T[:, :, :].rearrange("p c d -> p (c d)")
                    act.activation(dst[:, lo * P:hi * P], FILL_BANKS[n][:, 0:(hi - lo) * P], ACT.Copy)\
                       .then_inc(prep_drained, 1)

            def abs_sums(col, c, n, rows):
                act.activation(above12[rows, c:c + n, :].rearrange("p c d -> p (c d)"),
                               w12_n[rows, c:c + n, :].rearrange("p c d -> p (c d)"), ACT.Abs,
                               accum_out=abs_part[rows, col:col + 1]).then_inc(part_ready, 1)

            act.dma_start(xblk(0, 2, 2).rearrange("p (j d) -> p j d", j=2), x_dram[:, 0, 2:4]).then_inc(x_loaded, 16)
            act.dma_start(wo_n[:, :, :], w_o.rearrange("(c p) d -> p c d", p=P)).then_inc(wo_loaded, 16)
            act.dma_start(wat[:, 2 * KD:3 * KD, :], w_attn[2 * D:3 * D, :].rearrange("(c p) d -> p c d", p=P))\
               .then_inc(wv_loaded, 16)
            act.wait_ge(comp_full, 1)
            act.activation(m_hi[:, :, :].rearrange("p k d -> p (k d)"), d_bank[0][:, :], ACT.Copy).then_inc(comp_hi, 1)
            act.wait_ge(comp_full, 2)
            act.activation(woT[:, :, :].rearrange("p k d -> p (k d)"), d_bank[1][:, :], ACT.Copy).then_inc(wo_turned, 1)
            x_high(0)
            act.wait_ge(part_zeroed, 1)
            act.wait_ge(w1_loaded, 32)
            abs_sums(0, 0, HC, slice(0, P))
            act.wait_ge(comp_full, 3)
            act.activation(wvo_hi[:, :, :].rearrange("p k d -> p (k d)"), d_bank[0][:, :], ACT.Copy).then_inc(comp_hi, 1)
            abs_sums(1, 2 * HC, 1, slice(TAIL, P))
            z_high(0)
            act.wait_ge(w2_loaded, 32)
            abs_sums(PS, HC, HC, slice(0, P))
            u_high(0, (0,))
            abs_sums(PS + 1, 2 * HC, 1, slice(0, TAIL))
            u_high(0, (1,))
            x_high(1)
            squares(0, 0)
            squares(0, 1)
            z_high(1)
            drain_ternary((0, 1))
            act.wait_ge(w3_loaded, 16)
            for k in range(KD):
                act.activation(above3[:, k, 0:H], w3_n[:, k, :], ACT.Abs, accum_out=abs_part[:, 2 * PS + k:2 * PS + k + 1])\
                   .then_inc(part_ready, 1)
            u_high(1)
            drain_ternary((2,))
            x2_high(0)
            drain_ternary(range(3, len(FILLS12)))

            def step(a, f, ahead, begun=False):
                if not begun:
                    z_high(a)
                gates(f, 0)
                if not begun:
                    u_high(a, (0,))
                hid_high(f, 0)
                if not begun:
                    u_high(a, (1,))
                if begun:
                    drain_ternary((len(FILLS12), len(FILLS12) + 1))
                for n in (1, 2):
                    gates(f, n)
                    hid_high(f, n)
                    if begun and n == 1:
                        drain_ternary((len(FILLS12) + 2,))
                squares(a, 0)
                squares(a, 1)
                for n in (3, 4):
                    gates(f, n)
                    hid_high(f, n)
                gates(f, 5)
                if ahead:
                    x_high(a + 1)
                hid_high(f, 5)
                tail_stack(f)
                x2_high(a)

            step(1, 0, True, begun=True)
            with act.Fori(2, B - 1) as i:
                step(i, i - 1, True)
            step(B - 1, B - 2, False)
            last = B - 1
            for n in range(NU - 1):
                gates(last, n)
                if n < NU - 2:
                    hid_high(last, n)
            gates(last, NU - 1)
            hid_high(last, NU - 2)
            hid_high(last, NU - 1)
            tail_stack(last)

        @block.vector
        def _(dve):
            def block_stats(b, stats, stats_done, blocks=range(NB)):
                for j in blocks:
                    dve.bn_stats(stats[:, j, :], xblk(b, j)).then_inc(stats_done, 1)

            def moments(b, stats, stats_done, mv, mv_ready, blocks=range(NB)):
                wait_alone(dve, stats_done, b * NB + blocks[-1] + 1)
                for j in blocks:
                    dve.bn_aggr(mv[:, j, :], stats[:, j, :]).then_inc(mv_ready, 1)

            def normalise(b, mv, rstd, rstd_ready, piece, xn, xn_ready, blocks=range(NB)):
                dve.wait_ge(rstd_ready, piece)
                for j in blocks:
                    dve.tensor_scalar(xn[:, j, :], xblk(b, j), mv[:, j, 0:1], rstd[:, j:j + 1],
                                      ALU.subtract, ALU.mult).then_inc(xn_ready, 1)

            def low(b, stage, h, hi, dst):
                dve.wait_ge(a_hi, highs_of(b, stage, B - 1) + h + 1)
                dve.tensor_tensor(dst, bank_of(b, stage, h)[:, :], hi.bitcast(F32), ALU.subtract).then_inc(a_drained, 1)

            def x_low(b):
                for k in range(KD):
                    low(b, XT, k, xT_of(b)[0][:, k, :], xT_of(b)[1][:, k, :])

            def z_low(b, chunks=range(KD)):
                for m in chunks:
                    low(b, ZT, m, z_hi[:, m, :], z_lo[:, m, :])

            def u_low(b, halves=range(2)):
                for h in halves:
                    hs = slice(2 * h, 2 * h + 2)
                    low(b, UV, h, u_hi[:, hs, :].rearrange("p j d -> p (j d)"),
                        u_lo[:, hs, :].rearrange("p j d -> p (j d)"))

            def x2_low(b):
                for k in range(KD):
                    low(b, X2T, k, x2T_hi[:, k, :], x2T_lo[:, k, :])

            def mask(b, h):
                dve.wait_ge(a_full, turn_of(b, SC, B - 1) + h + 1)
                if not (isinstance(b, int) and b == 0):
                    dve.wait_ge(at_hi_ready, b * 2 + h - 1)
                cap = cap01[:, :, :, :].rearrange("p a c q -> p (a c q)") if h == 0 else \
                    cap23[:, :, :].rearrange("p a q -> p (a q)")
                cols = slice(0, 512) if h == 0 else slice(P, 512)
                dve.scalar_tensor_tensor(out=sc_pos[:, h, cols], in0=a_bank[h][:, cols], scalar=0.0, in1=cap,
                                         op0=ALU.max, op1=ALU.min).then_inc(a_drained, 1)

            def add_attention(b):
                for h in range(2):
                    dve.wait_ge(a_full, turn_of(b, YA, B - 1) + h + 1)
                    dve.tensor_tensor(xblk(b, 2 * h, 2), a_bank[h][:, :], xblk(b, 2 * h, 2), ALU.add).then_inc(a_drained, 1)
                    if h == 1:
                        moments(b, stats2, stats2_done, mv2, mv2_ready, (0, 1))
                    wait_alone(dve, a_drained, turn_of(b, YA, B - 1) + h + 1)
                    block_stats(b, stats2, stats2_done, (2 * h, 2 * h + 1))
                moments(b, stats2, stats2_done, mv2, mv2_ready, (2, 3))

            def hidden(b, n):
                dve.wait_ge(gate_ready, b * NU + n + 1)
                if not (isinstance(b, int) and b == 0 and n < 2):
                    dve.wait_ge(hid_lo_ready, b * NU + n - 1)
                if n == HC % 2 and not (isinstance(b, int) and b == 0):
                    dve.wait_ge(hid_hi_ready, b * (NU + 1))
                rows = slice(0, P) if n < HC else slice(0, TAIL)
                dve.tensor_tensor(hid[rows, n % 2, :], up_bank[n % 2][1 if n < HC else 0][rows, :], gate[rows, n % 2, :],
                                  ALU.mult).then_inc(hid_ready, 1)

            def add_ffn(b):
                for h in range(2):
                    dve.wait_ge(d_full, b * 2 + h + 1)
                    dve.tensor_tensor(xblk(b, 2 * h, 2), d_bank[h][:, :], xblk(b, 2 * h, 2), ALU.add).then_inc(out_ready, 1)

            dve.memset(abs_part[:, :], 0.0).then_inc(part_zeroed, 1)
            for h, loaded in enumerate((x0_half_loaded, x_loaded)):
                dve.wait_ge(loaded, 16)
                block_stats(0, stats1, stats1_done, (2 * h, 2 * h + 1))
                moments(0, stats1, stats1_done, mv1, mv1_ready, (2 * h, 2 * h + 1))
            for h in range(2):
                normalise(0, mv1, rstd1, rstd1_ready, h + 1, xn1, xn1_ready, (2 * h, 2 * h + 1))
            dve.wait_ge(comp_hi, 1)
            dve.tensor_tensor(m_lo[:, :, :].rearrange("p k d -> p (k d)"), d_bank[0][:, :],
                              m_hi[:, :, :].rearrange("p k d -> p (k d)").bitcast(F32), ALU.subtract).then_inc(comp_done, 1)
            x_low(0)
            dve.wait_ge(x_loaded, 32)
            block_stats(1, stats1, stats1_done)
            moments(1, stats1, stats1_done, mv1, mv1_ready)
            dve.wait_ge(comp_hi, 2)
            dve.tensor_tensor(wvo_lo[:, :, :].rearrange("p k d -> p (k d)"), d_bank[0][:, :],
                              wvo_hi[:, :, :].rearrange("p k d -> p (k d)").bitcast(F32), ALU.subtract).then_inc(comp_done, 1)
            def thresholds(w, tail_rows=None):
                dve.wait_ge(comp_full, 4 + w)
                dve.tensor_reduce(abs_total[:, w:w + 1], d_bank[1][:, w * PS:(w + 1) * PS], AX_X, ALU.add)\
                   .then_inc(total_ready, 1)
                dve.wait_ge(total_ready, w + 1)
                half_mean, half_eps = 0.5 / (H * D), 0.5 * QUANT_EPS
                for t, sign in ((thr, 1.0), (nthr, -1.0)):
                    for rows, c in [(slice(0, P), w)] + ([(tail_rows, 3)] if tail_rows else []):
                        dve.tensor_scalar(t[rows, c:c + 1], abs_total[rows, w:w + 1], sign * half_mean, sign * half_eps,
                                          ALU.mult, ALU.add).then_inc(thr_ready, 1)

            def compare(out, src, t, c, op):
                dve.tensor_scalar(out, src, t[:, c:c + 1], None, op).then_inc(ternary_ready, 1)

            z_low(0, (0,))
            thresholds(0, slice(TAIL, P))
            z_low(0, (1,))
            normalise(1, mv1, rstd1, rstd1_ready, 3, xn1, xn1_ready)
            u_low(0, (0,))
            dve.wait_ge(thr_ready, 4)
            compare(above12[:, 0:HC, :], w12_n[:, 0:HC, :], thr, 0, ALU.is_gt)
            u_low(0, (1,))
            x_low(1)
            dve.wait_ge(caps_ready, 4)
            mask(0, 0)
            thresholds(1, slice(0, TAIL))
            mask(0, 1)
            compare(below12[:, 0:HC, :], w12_n[:, 0:HC, :], nthr, 0, ALU.is_lt)
            dve.wait_ge(thr_ready, 8)
            compare(above12[:, HC:2 * HC, :], w12_n[:, HC:2 * HC, :], thr, 1, ALU.is_gt)
            z_low(1, (0,))
            compare(below12[:, HC:2 * HC, :], w12_n[:, HC:2 * HC, :], nthr, 1, ALU.is_lt)
            z_low(1, (1,))
            add_attention(0)
            thresholds(2)
            normalise(0, mv2, rstd2, rstd2_ready, 1, xn2, xn2_ready, (0, 1))
            normalise(0, mv2, rstd2, rstd2_ready, 2, xn2, xn2_ready, (2, 3))
            u_low(1)
            x2_low(0)
            dve.wait_ge(thr_ready, 10)
            compare(above3[:, :, 0:H], w3_n[:, :, :], thr, 2, ALU.is_gt)
            compare(above3[:, :, H:H3], w3_n[:, :, HC * P:H], thr, 2, ALU.is_gt)

            def step(a, f, ahead, begun=False):
                if not begun:
                    z_low(a)
                hidden(f, 0)
                if ahead:
                    wait_alone(dve, x_loaded, 16 * a + 32)
                    block_stats(a + 1, stats1, stats1_done)
                    moments(a + 1, stats1, stats1_done, mv1, mv1_ready)
                if not begun:
                    u_low(a)
                hidden(f, 1)
                if ahead:
                    normalise(a + 1, mv1, rstd1, rstd1_ready, a + 3, xn1, xn1_ready)
                hidden(f, 2)
                mask(a, 0)
                mask(a, 1)
                hidden(f, 3)
                hidden(f, 4)
                add_attention(a)
                normalise(a, mv2, rstd2, rstd2_ready, a * 2 + 1, xn2, xn2_ready, (0, 1))
                hidden(f, 5)
                normalise(a, mv2, rstd2, rstd2_ready, a * 2 + 2, xn2, xn2_ready, (2, 3))
                if ahead:
                    x_low(a + 1)
                x2_low(a)
                add_ffn(f)

            step(1, 0, True, begun=True)
            with dve.Fori(2, B - 1) as i:
                step(i, i - 1, True)
            step(B - 1, B - 2, False)
            last = B - 1
            for n in range(NU):
                hidden(last, n)
            for n in (NU - 2, NU - 1):
                dve.wait_ge(hid_hi_ready, last * (NU + 1) + n + 1)
                o, i, h = low_of(n)
                dve.tensor_tensor(o, i, h.bitcast(F32), ALU.subtract).then_inc(hid_lo_last, 1)
            add_ffn(last)

        @block.gpsimd
        def _(pool):
            def inv_std(piece, mv, mv_ready, count, veps, veps_ready, rstd, rstd_ready, blocks=slice(0, NB)):
                wait_alone(pool, mv_ready, count)
                pool.tensor_scalar(veps[:, blocks], mv[:, blocks, 1], LN_EPS, None, ALU.add).then_inc(veps_ready, 1)
                pool.wait_ge(veps_ready, piece + 1)
                pool.tensor_tensor(rstd[:, blocks], veps[:, blocks], neg_half[:, blocks], ALU.pow).then_inc(rstd_ready, 1)

            def inv_std1(b):
                inv_std(b + 1, mv1, mv1_ready, (b + 1) * NB, veps1, veps1_ready, rstd1, rstd1_ready)

            def inv_std2(b):
                for h in range(2):
                    inv_std(b * 2 + h, mv2, mv2_ready, b * NB + 2 * h + 2, veps2, veps2_ready, rstd2, rstd2_ready,
                            slice(2 * h, 2 * h + 2))

            def hid_low(b, n):
                pool.wait_ge(hid_hi_ready, b * (NU + 1) + n + 1)
                o, i, h = low_of(n)
                pool.tensor_tensor(o, i, h.bitcast(F32), ALU.subtract).then_inc(hid_lo_ready, 1)

            def at_low(b):
                for h in range(2):
                    cols = slice(0, 512) if h == 0 else slice(P, 512)
                    pool.wait_ge(sq_ready, b * 2 + h + 1)
                    pool.wait_ge(at_hi_ready, b * 2 + h + 1)
                    pool.tensor_tensor(at_lo[:, h, cols], sc_sq[:, h, cols], at_hi[:, h, cols].bitcast(F32),
                                       ALU.subtract).then_inc(at_lo_ready, 1)

            pool.memset(ident[:, :], 0.0).then_inc(zeroed, 1)
            pool.memset(neg_half[:, :], -0.5).then_inc(zeroed, 1)
            pool.memset(ones[:, :], 1.0).then_inc(zeroed, 1)
            pool.wait_ge(zeroed, 3)
            pool.affine_select(out=ident[:, :], in_=ident[:, :], compare_op=ALU.not_equal, fill=1.0, base=0,
                               pattern=[[-1, P]], channel_multiplier=1).then_inc(consts_ready, 1)
            for h in range(2):
                inv_std(h, mv1, mv1_ready, 2 * h + 2, veps1, veps1_ready, rstd1, rstd1_ready, slice(2 * h, 2 * h + 2))
            pool.memset(cap01[:, :, :, :], BIG).then_inc(zeroed, 1)
            pool.memset(cap23[:, :, :], BIG).then_inc(zeroed, 1)
            pool.wait_ge(zeroed, 5)
            same = dict(compare_op=ALU.is_ge, fill=0.0, base=0, channel_multiplier=-1)
            before = dict(compare_op=ALU.is_ge, fill=0.0, base=0, channel_multiplier=1)
            pool.affine_select(out=cap01[:, :, 0, :], in_=cap01[:, :, 0, :], pattern=[[0, 2], [1, P]], **same).then_inc(caps_ready, 1)
            pool.affine_select(out=cap01[:, :, 1, :], in_=cap01[:, :, 1, :], pattern=[[0, 2], [-1, P]], **before).then_inc(caps_ready, 1)
            pool.affine_select(out=cap23[:, 0:2, :], in_=cap23[:, 0:2, :], pattern=[[0, 2], [1, P]], **same).then_inc(caps_ready, 1)
            pool.affine_select(out=cap23[:, 2, :], in_=cap23[:, 2, :], pattern=[[-1, P]], **before).then_inc(caps_ready, 1)
            pool.wait_ge(consts_ready, 1)
            pool.tensor_copy(ident_bf[:, :], ident[:, :]).then_inc(consts_ready, 1)
            pool.tensor_scalar(nident_bf[:, :], ident[:, :], -1.0, None, ALU.mult).then_inc(consts_ready, 1)
            inv_std1(1)
            at_low(0)
            pool.wait_ge(thr_ready, 8)
            for t, out, op in ((thr, above12, ALU.is_gt), (nthr, below12, ALU.is_lt)):
                pool.tensor_scalar(out[:, 2 * HC, :], w12_n[:, 2 * HC, :], t[:, 3:4], None, op).then_inc(tails_ready, 1)
            inv_std2(0)
            pool.wait_ge(w3_loaded, 16)
            pool.wait_ge(thr_ready, 10)
            pool.tensor_scalar(below3[:, :, H:H3], w3_n[:, :, HC * P:H], nthr[:, 2:3], None, ALU.is_lt)\
                .then_inc(below3_ready, 1)
            pool.tensor_scalar(below3[:, :, 0:H], w3_n[:, :, :], nthr[:, 2:3], None, ALU.is_lt).then_inc(below3_ready, 1)

            def step(a, f, ahead):
                hid_low(f, 0)
                if ahead:
                    inv_std1(a + 1)
                hid_low(f, 1)
                hid_low(f, 2)
                at_low(a)
                hid_low(f, 3)
                hid_low(f, 4)
                inv_std2(a)
                hid_low(f, 5)

            step(1, 0, True)
            with pool.Fori(2, B - 1) as i:
                step(i, i - 1, True)
            step(B - 1, B - 2, False)
            for n in range(NU - 2):
                hid_low(B - 1, n)


_INS = ['L0_attn_x', 'L0_attn_w_attn', 'L0_attn_w_o', 'L0_ffn_w1', 'L0_ffn_w2', 'L0_ffn_w3']


def kernel(**inputs):
    import numpy as _np
    import concourse.bacc as _bacc
    from concourse import mybir as _mybir
    from concourse.bass_utils import run_bass_kernel_spmd as _run

    nc = _bacc.Bacc("TRN2", target_bir_lowering=False, num_devices=1)
    arrays, args = {}, []
    for name in _INS:
        a = _np.ascontiguousarray(inputs[name])
        arrays[f"in_{name}_dram"] = a
        args.append(nc.dram_tensor(f"in_{name}_dram", a.shape, _mybir.dt.from_np(a.dtype), kind="ExternalInput").ap())
    shape = inputs['L0_attn_x'].shape
    args.append(nc.dram_tensor("out_0_dram", shape, _mybir.dt.float32, kind="ExternalOutput").ap())
    build(nc, *args)
    r = _run(nc, [arrays], core_ids=[0])
    return r.results[0]["out_0_dram"]
```
